# Optimizing a Trainium2 kernel written in Bass

```python
import numpy as np
import jax
import jax.numpy as jnp

def _softmax(x, axis=-1):
    return jax.nn.softmax(x, axis=axis)

def _gelu(x):
    return jax.nn.gelu(x, approximate=True)

def _silu(x):
    return jax.nn.silu(x)

def _sigmoid(x):
    return jax.nn.sigmoid(x)

def _layernorm(x, axis=-1, eps=1e-05):
    m = jnp.mean(x, axis=axis, keepdims=True)
    v = jnp.var(x, axis=axis, keepdims=True)
    return (x - m) / jnp.sqrt(v + eps)

def _scatter_add(tgt, idx, src, axis=0):
    return tgt.at[idx].add(src)

def _segment_sum(src, seg, n):
    return jax.ops.segment_sum(src, seg, n)
kernel_name = 'mk_gnn_preln_d4_gnn_r32_c25317'

def setup_inputs(seed: int=0):
    np.random.seed(seed)
    _w = jnp.asarray

    def _rec_inputs():
        import jax
        import jax.numpy as jnp
        _gk = jax.random.key(seed)
        x = -0.0005121 + 1.001 * jax.random.normal(jax.random.fold_in(_gk, 1), (3125, 64), jnp.float32)
        _s = jax.random.randint(jax.random.fold_in(_gk, 2), (25000,), 0, 3125, jnp.int32)
        _d = jax.random.randint(jax.random.fold_in(_gk, 3), (25000,), 0, 3125, jnp.int32)
        _loop = jnp.arange(3125, dtype=jnp.int32)
        src = jnp.concatenate([_s, _d, _loop])
        dst = jnp.concatenate([_d, _s, _loop])
        _o = jnp.argsort(dst, stable=True)
        src = src[_o]
        dst = dst[_o]
        edge_type_8 = jax.random.randint(jax.random.fold_in(_gk, 13), (53125,), 0, 8, jnp.int32)
        edge_weight = jax.random.uniform(jax.random.fold_in(_gk, 14), (53125,), jnp.float32, 0.0, 0.999998)
        return (x, src, dst, edge_type_8, edge_weight)
    x, src, dst, edge_type_8, edge_weight = _rec_inputs()

    def _L0_gnn_setup():
        import jax, jax.numpy as jnp
        import numpy as np
        N_NODES = 50000
        N_EDGES = 25000
        FEAT_DIM = 64
        NUM_RELS = 8
        key = jax.random.key(seed)
        k1, k2, k3, k4, k5 = jax.random.split(key, 5)
        features = jax.random.normal(k1, (N_NODES, FEAT_DIM), dtype=jnp.float32)
        limit = np.sqrt(2.0) * np.sqrt(6.0 / (FEAT_DIM + FEAT_DIM))
        weight_r = jax.random.uniform(k2, (NUM_RELS, FEAT_DIM, FEAT_DIM), dtype=jnp.float32, minval=-limit, maxval=limit)
        src = jax.random.randint(k3, (N_EDGES,), 0, N_NODES, dtype=jnp.int64 if jax.config.jax_enable_x64 else jnp.int32)
        dst = jax.random.randint(k4, (N_EDGES,), 0, N_NODES, dtype=src.dtype)
        etype = jax.random.randint(k5, (N_EDGES,), 0, NUM_RELS, dtype=src.dtype)
        return {'features': features, 'weight_r': weight_r, 'src': src, 'dst': dst, 'etype': etype}
    _L0_gnn_all = _L0_gnn_setup()
    _L0_gnn_in = {k: v for k, v in _L0_gnn_all.items() if k in ('weight_r',)}
    del _L0_gnn_all

    def _L1_gnn_setup():
        import jax, jax.numpy as jnp
        import numpy as np
        N_NODES = 3125
        N_EDGES = 40000
        D = 64
        key = jax.random.key(seed)
        k1, k2, k3, k4, k5, k6 = jax.random.split(key, 6)
        feat = jax.random.normal(k1, (N_NODES, D), dtype=jnp.float32)
        W_attn = jax.random.normal(k2, (D, 2 * D), dtype=jnp.float32) * 0.1
        b_attn = jax.random.normal(k3, (D,), dtype=jnp.float32) * 0.1
        w_out = jax.random.normal(k4, (D,), dtype=jnp.float32) * 0.1
        src = jax.random.randint(k5, (N_EDGES,), 0, N_NODES, dtype=jnp.int32)
        dst = jax.random.randint(k6, (N_EDGES,), 0, N_NODES, dtype=jnp.int32)
        return {'feat': feat, 'W_attn': W_attn, 'b_attn': b_attn, 'w_out': w_out, 'src': src, 'dst': dst}
    _L1_gnn_all = _L1_gnn_setup()
    _L1_gnn_in = {k: v for k, v in _L1_gnn_all.items() if k in ('W_attn', 'b_attn', 'w_out')}
    del _L1_gnn_all

    def _L2_gnn_setup():
        import jax, jax.numpy as jnp
        import numpy as np
        N = 50000
        E = 25000
        C = 64
        K = 3

        def _sym_norm(edge_index, edge_weight, n, lambda_max=2.0):
            src = edge_index[0]
            dst = edge_index[1]
            deg = jax.ops.segment_sum(edge_weight, src, num_segments=n)
            safe = jnp.where(deg > 0, deg, 1.0)
            dis = jnp.where(deg > 0, 1.0 / jnp.sqrt(safe), 0.0)
            w = -dis[src] * edge_weight * dis[dst]
            return 2.0 / lambda_max * w

        def _propagate(x, src, dst, w, n):
            return jax.ops.segment_sum(w[:, None] * x[src], dst, num_segments=n)

        def _cheb_conv(x, src, dst, w, Wk, b, n):
            k_total = Wk.shape[0]
            Tx0 = x
            out = Tx0 @ Wk[0]
            Tx1 = _propagate(Tx0, src, dst, w, n)
            out = out + Tx1 @ Wk[1]
            for k in range(2, k_total):
                Tx2 = 2.0 * _propagate(Tx1, src, dst, w, n) - Tx0
                out = out + Tx2 @ Wk[k]
                Tx0, Tx1 = (Tx1, Tx2)
            return out + b
        key = jax.random.key(seed)
        ks = jax.random.split(key, 16)
        inp = {'X': jax.random.normal(ks[0], (N, C), dtype=jnp.float32), 'edge_index': jax.random.randint(ks[1], (2, E), 0, N, dtype=jnp.int64 if jax.config.jax_enable_x64 else jnp.int32), 'edge_weight': jax.random.uniform(ks[2], (E,), dtype=jnp.float32)}
        names = ['xz', 'hz', 'xr', 'hr', 'xh', 'hh']
        for i, nm in enumerate(names):
            inp['W' + nm] = jax.random.normal(ks[3 + 2 * i], (K, C, C), dtype=jnp.float32) * 0.1
            inp['b' + nm] = jax.random.normal(ks[4 + 2 * i], (C,), dtype=jnp.float32) * 0.1
        return inp
    _L2_gnn_all = _L2_gnn_setup()
    _L2_gnn_in = {k: v for k, v in _L2_gnn_all.items() if k in ('Wxz', 'bxz', 'Whz', 'bhz', 'Wxr', 'bxr', 'Whr', 'bhr', 'Wxh', 'bxh', 'Whh', 'bhh')}
    del _L2_gnn_all

    def _L3_gnn_setup():
        import jax, jax.numpy as jnp
        import numpy as np
        N_NODES = 3125
        key = jax.random.key(seed)
        k1, k2, k3, k4, k5, k6 = jax.random.split(key, 6)
        N, E, DIN, DOUT = (N_NODES, 50000, 64, 64)
        x = jax.random.normal(k1, (N, DIN), dtype=jnp.float32)
        edge_row = jax.random.randint(k2, (E,), 0, N, dtype=jnp.int64)
        edge_col = jax.random.randint(k3, (E,), 0, N, dtype=jnp.int64)
        edge_val = jax.random.uniform(k4, (E,), dtype=jnp.float32)
        stdv = 1.0 / np.sqrt(DOUT)
        weight = jax.random.uniform(k5, (DIN, DOUT), dtype=jnp.float32, minval=-stdv, maxval=stdv)
        bias = jax.random.uniform(k6, (DOUT,), dtype=jnp.float32, minval=-stdv, maxval=stdv)
        return {'x': x, 'edge_row': edge_row, 'edge_col': edge_col, 'edge_val': edge_val, 'weight': weight, 'bias': bias}
    _L3_gnn_all = _L3_gnn_setup()
    _L3_gnn_in = {k: v for k, v in _L3_gnn_all.items() if k in ('weight', 'bias')}
    del _L3_gnn_all
    return {'x': x, 'src': src, 'dst': dst, 'edge_type_8': edge_type_8, 'edge_weight': edge_weight, 'L0_gnn_weight_r': _L0_gnn_in['weight_r'], 'L1_gnn_W_attn': _L1_gnn_in['W_attn'], 'L1_gnn_b_attn': _L1_gnn_in['b_attn'], 'L1_gnn_w_out': _L1_gnn_in['w_out'], 'L2_gnn_Wxz': _L2_gnn_in['Wxz'], 'L2_gnn_bxz': _L2_gnn_in['bxz'], 'L2_gnn_Whz': _L2_gnn_in['Whz'], 'L2_gnn_bhz': _L2_gnn_in['bhz'], 'L2_gnn_Wxr': _L2_gnn_in['Wxr'], 'L2_gnn_bxr': _L2_gnn_in['bxr'], 'L2_gnn_Whr': _L2_gnn_in['Whr'], 'L2_gnn_bhr': _L2_gnn_in['bhr'], 'L2_gnn_Wxh': _L2_gnn_in['Wxh'], 'L2_gnn_bxh': _L2_gnn_in['bxh'], 'L2_gnn_Whh': _L2_gnn_in['Whh'], 'L2_gnn_bhh': _L2_gnn_in['bhh'], 'L3_gnn_weight': _L3_gnn_in['weight'], 'L3_gnn_bias': _L3_gnn_in['bias']}

def reference(x, src, dst, edge_type_8, edge_weight, L0_gnn_weight_r, L1_gnn_W_attn, L1_gnn_b_attn, L1_gnn_w_out, L2_gnn_Wxz, L2_gnn_bxz, L2_gnn_Whz, L2_gnn_bhz, L2_gnn_Wxr, L2_gnn_bxr, L2_gnn_Whr, L2_gnn_bhr, L2_gnn_Wxh, L2_gnn_bxh, L2_gnn_Whh, L2_gnn_bhh, L3_gnn_weight, L3_gnn_bias):
    import jax
    import jax.numpy as jnp

    def _L0_gnn_ref(features, weight_r, src, dst, etype):
        import jax, jax.numpy as jnp
        import numpy as np
        N_NODES = 50000
        N_EDGES = 25000
        FEAT_DIM = 64
        NUM_RELS = 8
        N, D = features.shape
        c = 0.2
        deg = jax.ops.segment_sum(jnp.ones(dst.shape, dtype=features.dtype), dst, num_segments=N)
        hw = jnp.einsum('nd,rdf->rnf', features, weight_r)
        msg = hw[etype, src] / deg[dst][:, None]
        M = jax.ops.segment_sum(msg, dst, num_segments=N)
        updated = jax.nn.relu(c * features + (1.0 - c) * M)
        return jnp.where((deg > 0)[:, None], updated, features)

    def _L1_gnn_ref(feat, W_attn, b_attn, w_out, src, dst):
        import jax, jax.numpy as jnp
        import numpy as np
        N_NODES = 3125
        N_EDGES = 40000
        D = 64
        N = feat.shape[0]
        h_src = feat[src]
        h_dst = feat[dst]
        hc = jnp.concatenate([h_src, h_dst], axis=-1)
        hc = jnp.tanh(hc @ W_attn.T + b_attn)
        e = hc @ w_out
        m = jax.ops.segment_max(e, dst, num_segments=N)
        m = jnp.where(jnp.isfinite(m), m, 0.0)
        ex = jnp.exp(e - m[dst])
        denom = jax.ops.segment_sum(ex, dst, num_segments=N)
        alpha = ex / jnp.where(denom == 0.0, 1.0, denom)[dst]
        z = jax.ops.segment_sum(alpha[:, None] * h_src, dst, num_segments=N)
        return z

    def _L2_gnn_ref(X, edge_index, edge_weight, Wxz, bxz, Whz, bhz, Wxr, bxr, Whr, bhr, Wxh, bxh, Whh, bhh):
        import jax, jax.numpy as jnp
        import numpy as np
        N = 50000
        E = 25000
        C = 64
        K = 3

        def _sym_norm(edge_index, edge_weight, n, lambda_max=2.0):
            src = edge_index[0]
            dst = edge_index[1]
            deg = jax.ops.segment_sum(edge_weight, src, num_segments=n)
            safe = jnp.where(deg > 0, deg, 1.0)
            dis = jnp.where(deg > 0, 1.0 / jnp.sqrt(safe), 0.0)
            w = -dis[src] * edge_weight * dis[dst]
            return 2.0 / lambda_max * w

        def _propagate(x, src, dst, w, n):
            return jax.ops.segment_sum(w[:, None] * x[src], dst, num_segments=n)

        def _cheb_conv(x, src, dst, w, Wk, b, n):
            k_total = Wk.shape[0]
            Tx0 = x
            out = Tx0 @ Wk[0]
            Tx1 = _propagate(Tx0, src, dst, w, n)
            out = out + Tx1 @ Wk[1]
            for k in range(2, k_total):
                Tx2 = 2.0 * _propagate(Tx1, src, dst, w, n) - Tx0
                out = out + Tx2 @ Wk[k]
                Tx0, Tx1 = (Tx1, Tx2)
            return out + b
        n = X.shape[0]
        src = edge_index[0]
        dst = edge_index[1]
        w = _sym_norm(edge_index, edge_weight, n)
        H = jnp.zeros((n, Wxz.shape[-1]), dtype=X.dtype)
        Z = jax.nn.sigmoid(_cheb_conv(X, src, dst, w, Wxz, bxz, n) + _cheb_conv(H, src, dst, w, Whz, bhz, n))
        R = jax.nn.sigmoid(_cheb_conv(X, src, dst, w, Wxr, bxr, n) + _cheb_conv(H, src, dst, w, Whr, bhr, n))
        H_tilde = jnp.tanh(_cheb_conv(X, src, dst, w, Wxh, bxh, n) + _cheb_conv(H * R, src, dst, w, Whh, bhh, n))
        return Z * H + (1.0 - Z) * H_tilde

    def _L3_gnn_ref(x, edge_row, edge_col, edge_val, weight, bias):
        import jax, jax.numpy as jnp
        import numpy as np
        N_NODES = 3125
        support = x @ weight
        msgs = edge_val[:, None] * support[edge_col]
        out = jax.ops.segment_sum(msgs, edge_row, num_segments=x.shape[0])
        return out + bias
    edge_index = jnp.stack([src, dst])
    h = jnp.maximum(_layernorm(x, axis=-1), 0.0)
    x = x + _L0_gnn_ref(h, L0_gnn_weight_r, src, dst, edge_type_8)
    h = jnp.maximum(_layernorm(x, axis=-1), 0.0)
    x = x + _L1_gnn_ref(h, L1_gnn_W_attn, L1_gnn_b_attn, L1_gnn_w_out, src, dst)
    h = jnp.maximum(_layernorm(x, axis=-1), 0.0)
    x = x + _L2_gnn_ref(h, edge_index, edge_weight, L2_gnn_Wxz, L2_gnn_bxz, L2_gnn_Whz, L2_gnn_bhz, L2_gnn_Wxr, L2_gnn_bxr, L2_gnn_Whr, L2_gnn_bhr, L2_gnn_Wxh, L2_gnn_bxh, L2_gnn_Whh, L2_gnn_bhh)
    h = jnp.maximum(_layernorm(x, axis=-1), 0.0)
    x = x + _L3_gnn_ref(h, src, dst, edge_weight, L3_gnn_weight, L3_gnn_bias)
    return x

_drawn_inputs = setup_inputs


def setup_inputs(seed=0):
    import zlib

    import numpy as np

    out = dict(_drawn_inputs(seed))
    spreads = {}
    factors = {'L1_gnn_b_attn': 163.205,
     'L2_gnn_bxz': 6.112,
     'L2_gnn_bhz': 5.632,
     'L1_gnn_W_attn': 3.091,
     'L1_gnn_w_out': 2.821}
    for name, (base, spread) in spreads.items():
        noise = np.random.default_rng([zlib.crc32(name.encode()), seed]).standard_normal(out[name].shape)
        drawn = base * np.exp(spread * noise) if base else spread * noise
        out[name] = jnp.asarray(drawn.astype(out[name].dtype))
    for name, factor in factors.items():
        out[name] = (out[name] * factor).astype(out[name].dtype)
    return out
```

```python
from contextlib import ExitStack

import concourse.bass as bass
from concourse import mybir
from concourse.alu_op_type import AluOpType as ALU

F32, I32, BF16 = mybir.dt.float32, mybir.dt.int32, mybir.dt.bfloat16
ACT = mybir.ActivationFunctionType
AX = mybir.AxisListType
PE_ENGINE = mybir.EngineType.PE


def gnn_kernel(nc, ins, out, layers=4):
    P = 128
    N, D = ins["x"].shape
    E = ins["src"].shape[0]
    R = ins["L0_gnn_weight_r"].shape[0]
    NB = -(-N // P)
    NFULL = N // P
    NREST = N - NFULL * P
    T = -(-E // P)
    H = 8
    IT = T // (2 * H)
    assert IT * 2 * H == T and N < NB * P
    TC = -(-T // P)
    TL = T - (TC - 1) * P
    EFULL = E // P
    EREST = E - EFULL * P
    W1 = D + 1
    BANK = 512
    BPB = BANK // W1
    ACC_BANKS = -(-(NB + 1) // BPB)
    NBA = ACC_BANKS * BPB
    EPS = 1e-5
    KEEP = 0.2
    GT = 4
    NG = -(-NB // GT)

    ctx = ExitStack()
    with ctx:
        def sb(name, shape, dt=F32):
            return ctx.enter_context(nc.sbuf_tensor(name, shape, dt))

        def ps(name, shape, dt=F32):
            return ctx.enter_context(nc.psum_tensor(name, shape, dt))

        def sem(name):
            return ctx.enter_context(nc.semaphore(name))

        relation_rows = nc.dram_tensor("relation_rows", [NB * P, R * D], F32).ap()
        attention_rows = nc.dram_tensor("attention_rows", [NB * P, 2 * D], F32).ap()
        cheb_rows = [nc.dram_tensor(f"cheb_rows{i}", [NB * P, D], F32).ap() for i in range(2)]
        sorted_rows = nc.dram_tensor("sorted_rows", [T * P, W1], F32).ap()
        local_rows = nc.dram_tensor("local_rows", [TC * P, P], BF16).ap()

        def carve(mem, at, shape, dt=F32):
            n = 1
            for x in shape:
                n *= x
            words = n // 2 if dt == BF16 else n
            view = mem[:, at:at + words]
            view = view if dt == F32 else view.bitcast(dt)
            if len(shape) == 2:
                view = view.rearrange("p (a b) -> p a b", a=shape[0])
            return view, at + words

        big = sb("big", [P, T * W1])
        edge_rows = big[:, :].rearrange("p (t c) -> p t c", t=T)
        relation_stage, at = carve(big, 0, [NB, R * D])
        hT0_view, at = carve(big, at, [NB * P])
        raw_dst, at = carve(big, at, [TC, P], I32)
        raw_src, at = carve(big, at, [TC, P], I32)
        raw_type, at = carve(big, at, [TC, P], I32)
        raw_weight, at = carve(big, at, [TC, P])
        src_hi_i, at = carve(big, at, [TC, P], I32)
        src_lo_i, at = carve(big, at, [TC, P], I32)
        row_vals = []
        for _ in range(4):
            view, at = carve(big, at, [TC, P])
            row_vals.append(view)
        row_src, row_rel, row_local, row_lo = row_vals
        local_bf, at = carve(big, at, [TC, P], BF16)
        idx_rel, at = carve(big, at, [T], I32)
        col_hi, at = carve(big, at, [T])
        col_lo, at = carve(big, at, [T])
        tile_block, at = carve(big, at, [T])
        tile_sum, at = carve(big, at, [T])
        tile_step, at = carve(big, at, [T])
        tile_ends, at = carve(big, at, [2, T])
        w_rel, at = carve(big, at, [R, D])
        w_rel = w_rel[0:D]
        assert at <= T * W1
        sums, _ = carve(big, NB * R * D + NB * P, [NBA, W1])
        pd, _ = carve(big, 0, [NB, D])
        pd_rest, _ = carve(big, NB * D, [NB, D])
        Tx1, _ = carve(big, 0, [NB, D])
        Tx2, _ = carve(big, NB * D, [NB, D])
        hT = []
        for i in range(3):
            view, _ = carve(big, NB * R * D, [NB * P]) if i == 0 else carve(big, (2 * D + (i - 1) * P) * NB, [NB * P])
            hT.append(view[0:D, :])
        assert (2 * D + 2 * P) * NB <= NB * R * D
        at = NB * (R * D + P) + NBA * W1
        keep_run, at = carve(big, at, [TC, P])
        in_block, at = carve(big, at, [TC, P])
        running, at = carve(big, at, [TC, P])
        picked, at = carve(big, at, [TC, P])
        place, at = carve(big, at, [TC, P])
        tile_counts, at = carve(big, at, [TC, NB + 1])
        place_base, at = carve(big, at, [TC, NB + 1])
        starts_here, at = carve(big, at, [TC, NB + 1])
        block_total, at = carve(big, at, [NB + 1])
        block_start, at = carve(big, at, [NB + 1])
        sorted_first, at = carve(big, at, [TC, 1])
        sorted_block, at = carve(big, at, [TC, 1])
        idx_place, at = carve(big, at, [T], I32)
        sorted_base, at = carve(big, at, [T])
        sorted_row, at = carve(big, at, [T])
        sorted_sum, at = carve(big, at, [T])
        sorted_step, at = carve(big, at, [T])
        sorted_at, at = carve(big, at, [T, 2], I32)
        assert at <= T * W1 and IT > NB

        idx_src = sb("idx_src", [P, T], I32)
        col_local = sb("col_local", [P, T])
        col_weight = sb("col_weight", [P, T])
        score = sb("score", [P, T])
        row_hi = sb("row_hi", [P, TC, P])
        weight_e = score
        same_flags = sb("same_flags", [P, TC * P + 1])
        same = same_flags[:, 0:TC * P]
        same_next = same_flags[:, 1:TC * P + 1]
        block_i = sb("block_i", [P, TC, 1], I32)
        block_f = sb("block_f", [P, TC, 1])
        block_first = sb("block_first", [P, TC, 1])
        ends = sb("ends", [P, TC, 2])
        sums_at = sb("sums_at", [1, T, 2], I32)
        pd_at = sb("pd_at", [1, T], I32)
        whole = sb("whole", [1, T])
        link = sb("link", [1, T])
        ident = sb("ident", [P, P])
        iota_row = sb("iota_row", [P, 2 * P])
        iota_part = sb("iota_part", [P, 2])
        zeros = sb("zeros", [P, BANK], BF16)
        before = sb("before", [P, P])
        ones = sb("ones", [P, P])
        local_src = [sb(f"local_src{h}", [P, H, 1]) for h in range(2)]
        w_attn = sb("w_attn", [D, 2 * D])
        w_attn_t = sb("w_attn_t", [D, 2, D])
        b_attn = sb("b_attn", [P, D])
        w_out = sb("w_out", [P, D])
        w_cheb = sb("w_cheb", [D, 3, 2, D])
        b_cheb = sb("b_cheb", [P, 2, 2, D])
        bias_cheb = sb("bias_cheb", [P, 2, D])
        w_gcn = sb("w_gcn", [D, D])
        b_gcn = sb("b_gcn", [P, D])
        X = sb("X", [P, NB, D])
        Hn = sb("Hn", [P, NB, D])
        stat = [sb(f"stat{i}", [P, NB, 1]) for i in range(6)]
        dis = sb("dis", [P, NB, 1])
        neg_dis = sb("neg_dis", [P, NB, 1])
        stage_mem = sb("stage_mem", [P, NB * 2 * D])
        stage = stage_mem[:, :].rearrange("p (b c) -> p b c", b=NB)
        xc, at = carve(stage_mem, 0, [NB, D])
        sq, _ = carve(stage_mem, at, [NB, D])
        shifted, at = carve(stage_mem, 0, [T])
        shift, at = carve(stage_mem, at, [T])
        expo, at = carve(stage_mem, at, [T])
        carry_f, at = carve(stage_mem, at, [2, T])
        carry_b, at = carve(stage_mem, at, [2, T])
        assert at <= NB * 2 * D
        carries = sb("carries", [1, 2, T])
        carry_cols = sb("carry_cols", [P, 2, TC])
        idx_ring = [sb(f"idx_ring{h}", [P, H], I32) for h in range(2)]
        row_ring = [sb(f"row_ring{h}", [P, H * 2 * D]) for h in range(2)]
        rows2 = [carve(row_ring[h], 0, [H, 2 * D])[0] for h in range(2)]
        rows = [carve(row_ring[h], 0, [H, W1])[0] for h in range(2)]
        hot_ring = [sb(f"hot_ring{h}", [P, H * (2 * P + P + NB)]) for h in range(2)]
        onehot, onehot_lo, onehot_hi = [], [], []
        onehot_t, local_ring, tanh_ring, prod_ring = [], [], [], []
        for h in range(2):
            for kept, shape in ((onehot, [H, 2 * P]), (onehot_lo, [H, P]), (onehot_hi, [H, NB])):
                view, at = carve(hot_ring[h], 0 if kept is onehot else at, shape)
                kept.append(view)
            for kept, shape, dt in ((onehot_t, [2, H * P], BF16), (local_ring, [H * P], BF16),
                                    (tanh_ring, [H, D], F32), (prod_ring, [H, D], F32)):
                view, at = carve(hot_ring[h], 0 if kept is onehot_t else at, shape, dt)
                kept.append(view)
        V, at = carve(hot_ring[0], 0, [TC, P])
        prefix, at = carve(hot_ring[0], at, [TC, P])
        suffix, at = carve(hot_ring[0], at, [TC, P])
        attend_dst = sb("attend_dst", [P, 3, (NB + 1) * D], BF16)
        above = sb("above", [P, 1])
        w_abs = sb("w_abs", [P, D])

        acc = ps("acc", [P, ACC_BANKS * BANK])
        work = [ps(f"work{i}", [P, BANK]) for i in range(4)]

        raw_cleared = sem("raw_cleared")
        x_cleared = sem("x_cleared")
        consts_ready = sem("consts_ready")
        raw_loaded = sem("raw_loaded")
        x_loaded = sem("x_loaded")
        params_loaded = sem("params_loaded")
        rows_derived = sem("rows_derived")
        local_stored = sem("local_stored")
        prep_turned = sem("prep_turned")
        prep_taken = sem("prep_taken")
        tile_rows_turned = sem("tile_rows_turned")
        tile_info_ready = sem("tile_info_ready")
        attn_w_turned = sem("attn_w_turned")
        attn_w_taken = sem("attn_w_taken")
        var_ready = sem("var_ready")
        std_ready = sem("std_ready")
        h_ready = sem("h_ready")
        turned = sem("turned")
        turn_taken = sem("turn_taken")
        mm_done = [sem(f"mm_done{k}") for k in range(4)]
        mm_taken = [sem(f"mm_taken{k}") for k in range(4)]
        table_staged = sem("table_staged")
        passes = ["rel", "att", "ch0", "ch1"]
        table_stored = {k: sem(f"table_stored_{k}") for k in passes}
        idx_copied = {k: sem(f"idx_copied_{k}") for k in passes}
        gathered = {k: [sem(f"gathered_{k}{h}") for h in range(2)] for k in passes}
        FREED = 2 * IT + 2
        sum_passes = ["rel", "agg", "ch0", "ch1", "gcn"]
        slot_free = {k: sem(f"slot_free_{k}") for k in [*sum_passes, "att", "msg"]}
        onehot_ready = {k: sem(f"onehot_ready_{k}") for k in [*sum_passes, "att", "msg"]}
        sums_taken = {k: sem(f"sums_taken_{k}") for k in sum_passes}
        local_here3 = [sem(f"local_here3{h}") for h in range(2)]
        rank_step = sem("rank_step")
        place_step = sem("place_step")
        tile_counts_ready = sem("tile_counts_ready")
        bases_ready = sem("bases_ready")
        places_ready = sem("places_ready")
        places_turned = sem("places_turned")
        msgs_ready = sem("msgs_ready")
        place_copied = sem("place_copied")
        scattered = [sem(f"scattered{h}") for h in range(2)]
        sorted_here = [sem(f"sorted_here{h}") for h in range(2)]
        local_src_ready = sem("local_src_ready")
        local_here = [sem(f"local_here{h}") for h in range(2)]
        pd_ready = sem("pd_ready")
        preact_ready = sem("preact_ready")
        tanh_ready = sem("tanh_ready")
        rows_kept = sem("rows_kept")
        prod_ready = sem("prod_ready")
        hi_ready = sem("hi_ready")
        scores_ready = sem("scores_ready")
        shifted_ready = sem("shifted_ready")
        scores_turned = sem("scores_turned")
        edge_vals_ready = sem("edge_vals_ready")
        edge_vals_turned = sem("edge_vals_turned")
        carries_ready = sem("carries_ready")
        carries_turned = sem("carries_turned")
        max_ready = sem("max_ready")
        max_turned = sem("max_turned")
        expo_ready = sem("expo_ready")
        weight_ready = sem("weight_ready")
        gates_ready = sem("gates_ready")
        gates_done = sem("gates_done")
        vec = sem("vec")
        out_ready = sem("out_ready")
        out_stored = sem("out_stored")

        RAW_LOADS = 4 * 3
        block = ctx.enter_context(nc.Block())

        def blocks_of(table):
            return table.rearrange("(b p) c -> p b c", p=P)

        @block.sync
        def _(sp):
            def broadcast_local(key, here):
                with sp.Fori(0, IT) as it:
                    for h in range(2):
                        sp.wait_ge(slot_free[key], it * 2 + h + 1)
                        sp.dma_start(local_ring[h][:, :],
                                     local_rows[bass.ds(it * (2 * H) + h * H, H), :].rearrange("(a t) p -> a (t p)", a=1)
                                     .to_broadcast([P, H * P])).then_inc(here[h], 16)

            fulls = (TC - 1) * P
            pairs = ((raw_dst, "dst"), (raw_src, "src"), (raw_type, "edge_type_8"), (raw_weight, "edge_weight"))
            for tile, name in pairs:
                sp.dma_start(tile[:, 0:TC - 1, :], ins[name][0:fulls * P].rearrange("(c t p) -> t c p", t=P, p=P)
                             ).then_inc(raw_loaded, 16)
            sp.wait_ge(raw_cleared, 4)
            for tile, name in pairs:
                sp.dma_start(tile[0:EFULL - fulls, TC - 1, :],
                             ins[name][fulls * P:EFULL * P].rearrange("(t p) -> t p", p=P)).then_inc(raw_loaded, 16)
                sp.dma_start(tile[EFULL - fulls:EFULL - fulls + 1, TC - 1, 0:EREST],
                             ins[name][EFULL * P:E].rearrange("(t p) -> t p", t=1)).then_inc(raw_loaded, 16)
            sp.dma_start(X[:, 0:NFULL, :], ins["x"][0:NFULL * P, :].rearrange("(b p) d -> p b d", p=P)
                         ).then_inc(x_loaded, 16)
            sp.wait_ge(x_cleared, 1)
            sp.dma_start(X[0:NREST, NFULL, :], ins["x"][NFULL * P:N, :]).then_inc(x_loaded, 16)
            sp.dma_start(w_rel[:, :, :], ins["L0_gnn_weight_r"].rearrange("r d f -> d r f")).then_inc(params_loaded, 16)
            sp.dma_start(w_attn[:, :], ins["L1_gnn_W_attn"]).then_inc(params_loaded, 16)
            for k in range(3):
                for g, name in enumerate(("L2_gnn_Wxz", "L2_gnn_Wxh")):
                    sp.dma_start(w_cheb[:, k, g, :], ins[name][k, :, :]).then_inc(params_loaded, 16)
            sp.dma_start(w_gcn[:, :], ins["L3_gnn_weight"]).then_inc(params_loaded, 16)
            vectors = [(b_attn[:, :], "L1_gnn_b_attn"), (w_out[:, :], "L1_gnn_w_out"), (b_gcn[:, :], "L3_gnn_bias")]
            vectors += [(b_cheb[:, i // 2, i % 2, :], "L2_gnn_" + n) for i, n in enumerate(("bxz", "bxh", "bhz", "bhh"))]
            for tile, name in vectors:
                sp.dma_start(tile, ins[name].rearrange("(a d) -> a d", a=1).to_broadcast([P, D])
                             ).then_inc(params_loaded, 16)
            sp.wait_ge(rows_derived, 1)
            sp.dma_start(local_rows.rearrange("(c t) p -> t c p", t=P), local_bf[:, :, :]).then_inc(local_stored, 16)

            for j in range(5):
                s = slice(j * NB // 5, (j + 1) * NB // 5)
                sp.wait_ge(mm_taken[0], s.stop)
                sp.dma_start(blocks_of(relation_rows)[:, s, :], relation_stage[:, s, :]).then_inc(table_stored["rel"], 16)

            if layers > 1:
                sp.wait_ge(table_staged, 1)
                sp.dma_start(blocks_of(attention_rows), stage[:, :, :]).then_inc(table_stored["att"], 16)
                sp.wait_ge(local_stored, 16)
                broadcast_local("att", local_here)
            for i, k in enumerate(("ch0", "ch1")):
                if layers > 2:
                    sp.wait_ge(table_staged, 2 + i)
                    sp.dma_start(blocks_of(cheb_rows[i]), stage[:, :, 0:D]).then_inc(table_stored[k], 16)
            if layers > 3:
                sp.wait_ge(sums_taken["ch1"], 1)
                broadcast_local("msg", local_here3)
                for h in range(2):
                    sp.wait_ge(scattered[h], IT * 16 * H)
                with sp.Fori(0, IT) as it:
                    for h in range(2):
                        sp.wait_ge(slot_free["gcn"], it * 2 + h + 1)
                        sp.dma_start(rows[h][:, :, :], sorted_rows[bass.ds(it * (2 * H * P) + h * (H * P), H * P), :]
                                     .rearrange("(t p) c -> p t c", p=P)).then_inc(sorted_here[h], 16)
            sp.wait_ge(out_ready, 1)
            sp.dma_start(out[0:NFULL * P, :].rearrange("(b p) d -> p b d", p=P), X[:, 0:NFULL, :]).then_inc(out_stored, 16)
            sp.dma_start(out[NFULL * P:N, :], X[0:NREST, NFULL, :]).then_inc(out_stored, 16)
            sp.wait_ge(out_stored, 32)

        @block.gpsimd
        def _(pool):
            last = TC - 1
            pool.memset(raw_dst[:, last, :], 1 << 14).then_inc(raw_cleared, 1)
            pool.memset(raw_src[:, last, :], NB * P - 1).then_inc(raw_cleared, 1)
            pool.memset(raw_type[:, last, :], 0).then_inc(raw_cleared, 1)
            pool.memset(raw_weight[:, last, :], 0.0).then_inc(raw_cleared, 1)
            pool.memset(X[:, NFULL, :], 0.0).then_inc(x_cleared, 1)
            pool.memset(ident[:, :], 0.0).then_inc(consts_ready, 1)
            pool.iota(iota_row[:, :], [[1, 2 * P]], base=0, channel_multiplier=0,
                      allow_small_or_imprecise_dtypes=True).then_inc(consts_ready, 1)
            pool.iota(iota_part[:, :], [[P, 2]], base=0, channel_multiplier=1,
                      allow_small_or_imprecise_dtypes=True).then_inc(consts_ready, 1)
            pool.memset(zeros[:, :], 0.0).then_inc(consts_ready, 1)
            pool.wait_ge(consts_ready, 4)
            pool.affine_select(out=ident[:, :], in_=ident[:, :], compare_op=ALU.not_equal, fill=1.0,
                               base=0, pattern=[[-1, P]], channel_multiplier=1).then_inc(consts_ready, 1)
            pool.memset(ones[:, :], 1.0).then_inc(consts_ready, 1)
            pool.wait_ge(consts_ready, 6)
            pool.affine_select(out=before[:, :], in_=ones[:, :], compare_op=ALU.is_gt, fill=0.0,
                               base=0, pattern=[[1, P]], channel_multiplier=-1).then_inc(consts_ready, 1)
            for h in range(2):
                pool.memset(rows[h][:, :, D:W1], 1.0).then_inc(consts_ready, 1)
            pool.memset(attend_dst[:, :, NB * D:], 0.0).then_inc(consts_ready, 1)
            pool.memset(same_flags[:, TC * P:TC * P + 1], 0.0).then_inc(consts_ready, 1)

            def gather(key, table, index, ring, width, stores):
                pool.wait_ge(table_stored[key], 16 * stores)
                with pool.Fori(0, IT) as it:
                    for h in range(2):
                        pool.wait_ge(slot_free[key], it * 2 + h + 1)
                        pool.tensor_copy(idx_ring[h][:, :], index[:, bass.ds(it * (2 * H) + h * H, H)]
                                         ).then_inc(idx_copied[key], 1)
                        pool.wait_ge(idx_copied[key], it * 2 + h + 1)
                        pool.nop(nofuse=True)
                        for u in range(H):
                            pool.indirect_dma_start(
                                ring[h][:, u, 0:width], None, table,
                                bass.IndirectOffsetOnAxis(ap=idx_ring[h][:, u:u + 1], axis=0),
                            ).then_inc(gathered[key][h], 16)

            pool.wait_ge(prep_taken, 6)
            gather("rel", relation_rows.rearrange("n (r f) -> (n r) f", r=R), idx_rel, rows, D, 5)
            if layers > 1:
                gather("att", attention_rows, idx_src, rows2, 2 * D, 1)
            if layers > 2:
                gather("ch0", cheb_rows[0], idx_src, rows, D, 1)
                gather("ch1", cheb_rows[1], idx_src, rows, D, 1)
            if layers > 3:
                pool.wait_ge(places_ready, 4)
                with pool.Fori(0, IT) as it:
                    for h in range(2):
                        pool.wait_ge(msgs_ready, it * 2 + h + 3)
                        pool.tensor_copy(idx_ring[h][:, :], idx_place[:, bass.ds(it * (2 * H) + h * H, H)]
                                         ).then_inc(place_copied, 1)
                        pool.wait_ge(place_copied, it * 2 + h + 1)
                        pool.nop(nofuse=True)
                        for u in range(H):
                            pool.indirect_dma_start(
                                sorted_rows, bass.IndirectOffsetOnAxis(ap=idx_ring[h][:, u:u + 1], axis=0),
                                rows[h][:, u, :], None).then_inc(scattered[h], 16)

        @block.scalar
        def _(act):
            def std(k):
                act.wait_ge(var_ready, k + 1)
                act.activation(stat[3][:, :, :], stat[2][:, :, :], ACT.Sqrt).then_inc(std_ready, 1)

            def take_turned(s, buf):
                for g in range(NG):
                    n = s * NG + g
                    w = min(GT, NB - g * GT) * P
                    act.wait_ge(turned, n + 1)
                    act.activation(hT[buf][:, g * GT * P:g * GT * P + w], work[n % 2][0:D, 0:w], ACT.Copy
                                   ).then_inc(turn_taken, 1)

            std(0)
            take_turned(0, 0)
            act.wait_ge(var_ready, 2)
            act.activation(stat[3][:, :, :], stat[2][:, :, :], ACT.Sqrt).then_inc(std_ready, 1)
            if layers > 1:
                std(2)
                take_turned(1, 0)
                act.wait_ge(pd_ready, 1)
                with act.Fori(0, IT) as it:
                    for h in range(2):
                        act.wait_ge(gathered["att"][h], (it + 1) * (16 * H))
                        act.activation(edge_rows[:, bass.ds(it * (2 * H) + h * H, H), 0:D], rows2[h][:, :, D:2 * D],
                                       ACT.Copy).then_inc(rows_kept, 1)
                        act.wait_ge(prod_ready, it * 2 + h + 1)
                        act.wait_ge(preact_ready, it * 2 + h + 1)
                        act.activation(tanh_ring[h][:, :, :].rearrange("p t d -> p (t d)"), work[2 + h][:, :], ACT.Tanh
                                       ).then_inc(tanh_ready, 1)
                act.wait_ge(expo_ready, 1)
                act.activation(weight_e[:, :], expo[:, :], ACT.Exp).then_inc(weight_ready, 1)
            if layers > 2:
                std(3)
                for s in (2, 3, 4):
                    take_turned(s, s - 2)
                act.wait_ge(gates_ready, 1)
                act.activation(Tx1[:, :, :], stage[:, :, 0:D], ACT.Sigmoid, scale=-1.0).then_inc(gates_done, 1)
                act.activation(Tx2[:, :, :], stage[:, :, D:2 * D], ACT.Tanh).then_inc(gates_done, 1)
            if layers > 3:
                std(4)
                take_turned(5, 0)

        @block.tensor
        def _(pe):
            def turn(s, src):
                pe.wait_ge(h_ready, s + 1)
                for g in range(NG):
                    n = s * NG + g
                    if n >= 2:
                        pe.wait_ge(turn_taken, n - 1)
                    for b in range(g * GT, min((g + 1) * GT, NB)):
                        c = (b - g * GT) * P
                        t = pe.transpose(work[n % 2][0:D, c:c + P], src[:, b, :], ident[:, :])
                    t.then_inc(turned, 1)

            def clear_sums(key, wait=None):
                if wait is not None:
                    pe.wait_ge(wait, 1)
                for i in range(ACC_BANKS):
                    m = pe.matmul(acc[:, i * BANK:(i + 1) * BANK], zeros[:, 0:P], zeros[:, :],
                                  start=True, stop=False, skip_group_check=True)
                    if i >= ACC_BANKS - 2:
                        m.then_inc(slot_free[key], 1)

            def add_up(key, rows_of, width, ready, where=sums_at):
                with pe.Fori(0, IT) as it:
                    for h in range(2):
                        _, at = nc.values_load_multi_w_load_instructions(
                            where[0:1, :, :].rearrange("a t w -> a (t w)")[:, bass.ds(it * (4 * H) + h * (2 * H), 2 * H)],
                            engines=[PE_ENGINE], min_val=0, max_val=(ACC_BANKS - 1) * BANK + (BPB - 1) * W1,
                            skip_runtime_bounds_check_because="a node's block, below NB, and the block after it")
                        pe.wait_ge(onehot_ready[key], it * 2 + h + 1)
                        if ready is not None:
                            pe.wait_ge(ready[h], (it + 1) * (16 if key == "gcn" else 16 * H))
                        for u in range(H):
                            for w in range(2):
                                m = pe.matmul(acc[:, bass.ds(at[2 * u + w], width)], onehot[h][:, u, w * P:(w + 1) * P],
                                              rows_of(it, h, u), start=False, stop=False, skip_group_check=True)
                        if key == "rel":
                            for u in range(H):
                                m = pe.matmul(work[0][:, 0:NB], onehot_lo[h][:, u, :], onehot_hi[h][:, u, :],
                                              start=False, stop=False, skip_group_check=True)
                        m.then_inc(slot_free[key], 1)

            def look_up(key, source_rows):
                for h in range(2):
                    pe.matmul(work[2 + h][:, :], zeros[:, 0:P], zeros[:, :], start=True, stop=True
                              ).then_inc(slot_free[key], 1)
                with pe.Fori(0, IT) as it:
                    for h in range(2):
                        _, at = nc.values_load_multi_w_load_instructions(
                            pd_at[0:1, bass.ds(it * (2 * H) + h * H, H)], engines=[PE_ENGINE],
                            min_val=0, max_val=(NB - 1) * D,
                            skip_runtime_bounds_check_because="a node's block, below NB")
                        pe.wait_ge(onehot_ready[key], it * 2 + h + 1)
                        if source_rows is None:
                            pe.wait_ge(msgs_ready, it * 2 + h + 1)
                        else:
                            pe.wait_ge(source_rows[h], (it + 1) * (16 * H))
                        for u in range(H):
                            for w in range(2):
                                for part in range(3):
                                    m = pe.matmul(work[2 + h][:, u * D:(u + 1) * D],
                                                  onehot_t[h][:, w, u * P:(u + 1) * P],
                                                  attend_dst[:, part, bass.ds(at[u] + w * D, D)],
                                                  start=(w == 0 and part == 0), stop=False, skip_group_check=True)
                            if source_rows is not None:
                                m = pe.matmul(work[2 + h][:, u * D:(u + 1) * D], ident[:, :], rows2[h][:, u, 0:D],
                                              start=False, stop=True, skip_group_check=True)
                        if source_rows is None:
                            m.then_inc(slot_free[key], 1)
                        else:
                            m.then_inc(preact_ready, 1)
                            pe.wait_ge(preact_ready, it * 2 + h + 1)
                            pe.wait_ge(rows_kept, it * 2 + h + 1)
                            pe.sem_inc(slot_free[key], 1)

            pe.wait_ge(consts_ready, 7)
            turned_rows = [row_src, row_rel, row_local, row_hi, row_lo, raw_weight]
            for i, r in enumerate(turned_rows):
                pe.wait_ge(rows_derived, 2)
                if i >= 2:
                    pe.wait_ge(prep_taken, i - 1)
                for c in range(TC):
                    k = P if c < TC - 1 else TL
                    t = pe.transpose(work[i % 2][:, c * P:c * P + k], r[0:k, c, :], ident[0:k, 0:k])
                t.then_inc(prep_turned, 1)
            pe.wait_ge(prep_taken, 6)
            for i, r in enumerate((block_f[:, :, 0:1], ends[:, :, 0:1], ends[:, :, 1:2])):
                for c in range(TC):
                    k = P if c < TC - 1 else TL
                    t = pe.matmul(work[i][0:1, c * P:c * P + k], r[0:k, c, :], ident[0:k, 0:k], start=True, stop=True)
                t.then_inc(tile_rows_turned, 1)
            pe.wait_ge(params_loaded, 16 * 16)
            for i in range(2):
                t = pe.transpose(work[3][0:D, i * D:(i + 1) * D], w_attn[:, i * D:(i + 1) * D], ident[0:D, 0:D])
            t.then_inc(attn_w_turned, 1)

            pe.wait_ge(tile_info_ready, 1)
            pe.wait_ge(attn_w_taken, 1)
            turn(0, Hn)
            for b in range(NB):
                pe.wait_ge(turn_taken, b // GT + 1)
                if b >= 2:
                    pe.wait_ge(mm_taken[0], b - 1)
                pe.matmul(work[2 + b % 2][:, 0:R * D], hT[0][:, b * P:(b + 1) * P],
                          w_rel[:, :, :].rearrange("d r f -> d (r f)"), start=True, stop=True).then_inc(mm_done[0], 1)
            pe.matmul(work[0][:, 0:NB], zeros[:, 0:P], zeros[:, 0:NB], start=True, stop=False, skip_group_check=True)
            clear_sums("rel")
            add_up("rel", lambda it, h, u: rows[h][:, u, :], W1, gathered["rel"])
            if layers > 1:
                turn(1, Hn)
                for g in range(NG):
                    pe.wait_ge(turn_taken, NG + g + 1)
                    if g >= 2:
                        pe.wait_ge(mm_taken[1], g - 1)
                    for b in range(g * GT, min((g + 1) * GT, NB)):
                        c = (b - g * GT) * P
                        m = pe.matmul(work[2 + g % 2][:, c:c + 2 * D], hT[0][:, b * P:(b + 1) * P],
                                      w_attn_t[:, :, :].rearrange("d a j -> d (a j)"), start=True, stop=True)
                    m.then_inc(mm_done[1], 1)
                pe.wait_ge(pd_ready, 1)
                pe.wait_ge(mm_taken[1], NG)
                look_up("att", gathered["att"])
                pe.wait_ge(shifted_ready, 1)
                for c in range(TC):
                    k = P if c < TC - 1 else TL
                    t = pe.transpose(work[0][0:k, c * P:(c + 1) * P], shifted[:, c * P:c * P + k], ident[:, :])
                t.then_inc(scores_turned, 1)
                pe.wait_ge(edge_vals_ready, 1)
                for i, r in enumerate((prefix[:, :, P - 1:P], suffix[:, :, 0:1])):
                    for c in range(TC):
                        k = P if c < TC - 1 else TL
                        t = pe.matmul(work[2 + i][0:1, c * P:c * P + k], r[0:k, c, :], ident[0:k, 0:k],
                                      start=True, stop=True)
                t.then_inc(edge_vals_turned, 1)
                pe.wait_ge(carries_ready, 1)
                for i in range(2):
                    for c in range(TC):
                        k = P if c < TC - 1 else TL
                        t = pe.matmul(work[1][0:k, i * TC + c:i * TC + c + 1], carries[0:1, i, c * P:c * P + k],
                                      ident[0:1, 0:1], start=True, stop=True)
                t.then_inc(carries_turned, 1)
                pe.wait_ge(max_ready, 1)
                for c in range(TC):
                    k = P if c < TC - 1 else TL
                    t = pe.transpose(work[2][:, c * P:c * P + k], prefix[0:k, c, :], ident[0:k, 0:k])
                t.then_inc(max_turned, 1)
                clear_sums("agg", sums_taken["rel"])
                add_up("agg", lambda it, h, u: edge_rows[:, bass.ds(it * (2 * H) + (h * H + u), 1), :]
                       .rearrange("p a c -> p (a c)"), W1, None)

            if layers > 2:
                for i, (key, mat) in enumerate((("ch0", Hn), ("ch1", Tx1))):
                    if i == 1:
                        pe.wait_ge(tile_counts_ready, 1)
                        w = NB + 1
                        for c in range(TC):
                            k = P if c < TC - 1 else TL
                            pe.matmul(work[2][:, c * w:(c + 1) * w], before[0:k, :], tile_counts[0:k, c, :],
                                      start=True, stop=(c == 0), skip_group_check=True)
                            for d in range(c):
                                pe.matmul(work[2][:, c * w:(c + 1) * w], ones[:, :], tile_counts[:, d, :],
                                          start=False, stop=(d == c - 1), skip_group_check=True)
                        for c in range(TC):
                            k = P if c < TC - 1 else TL
                            m = pe.matmul(work[3][:, 0:w], ones[0:k, :], tile_counts[0:k, c, :],
                                          start=(c == 0), stop=(c == TC - 1))
                        m.then_inc(bases_ready, 1)
                    turn(2 + i, mat)
                    clear_sums(key, sums_taken[("agg", "ch0")[i]])
                    add_up(key, lambda it, h, u: rows[h][:, u, 0:D], D, gathered[key])
                pe.wait_ge(places_ready, 1)
                for c in range(TC):
                    k = P if c < TC - 1 else TL
                    t = pe.transpose(work[2][:, c * P:c * P + k], place[0:k, c, :], ident[0:k, 0:k])
                for c in range(TC):
                    k = P if c < TC - 1 else TL
                    t = pe.matmul(work[3][0:1, c * P:c * P + k], sorted_block[0:k, c, :], ident[0:k, 0:k],
                                  start=True, stop=True)
                t.then_inc(places_turned, 1)
                pe.wait_ge(places_ready, 4)
                pe.matmul(work[2][:, 0:T], ones[0:1, :], sorted_row[0:1, :], start=True, stop=True
                          ).then_inc(places_turned, 1)
                pe.wait_ge(places_ready, 5)
                turn(4, Tx2)
                for g in range(NG):
                    pe.wait_ge(turn_taken, 4 * NG + g + 1)
                    if g >= 2:
                        pe.wait_ge(mm_taken[2], g - 1)
                    for b in range(g * GT, min((g + 1) * GT, NB)):
                        c = (b - g * GT) * P
                        for k in range(3):
                            m = pe.matmul(work[2 + g % 2][:, c:c + 2 * D], hT[k][:, b * P:(b + 1) * P],
                                          w_cheb[:, k, :, :].rearrange("d g f -> d (g f)"), start=(k == 0), stop=(k == 2))
                    m.then_inc(mm_done[2], 1)

            if layers > 3:
                turn(5, Hn)
                for g in range(NG):
                    pe.wait_ge(turn_taken, 5 * NG + g + 1)
                    if g >= 2:
                        pe.wait_ge(mm_taken[3], g - 1)
                    for b in range(g * GT, min((g + 1) * GT, NB)):
                        c = (b - g * GT) * D
                        m = pe.matmul(work[2 + g % 2][:, c:c + D], hT[0][:, b * P:(b + 1) * P], w_gcn[:, :],
                                      start=True, stop=True)
                    m.then_inc(mm_done[3], 1)
                pe.wait_ge(pd_ready, 2)
                look_up("msg", None)
                clear_sums("gcn", sums_taken["ch1"])
                add_up("gcn", lambda it, h, u: rows[h][:, u, 0:D], D, sorted_here, sorted_at)

        @block.vector
        def _(dve):
            steps = [0]

            def then(ins):
                steps[0] += 1
                ins.then_inc(vec, 1)
                dve.wait_ge(vec, steps[0])

            def per_node(a):
                return a[:, :, :].to_broadcast([P, NB, D])

            def layernorm(k, sqrt_no):
                then(dve.tensor_reduce(stat[0][:, :, :], X[:, :, :], AX.X, ALU.add))
                then(dve.tensor_single_scalar(stat[1][:, :, :], stat[0][:, :, :], 1.0 / D, ALU.mult))
                then(dve.tensor_tensor(xc[:, :, :], X[:, :, :], per_node(stat[1]), ALU.subtract))
                then(dve.tensor_tensor(sq[:, :, :], xc[:, :, :], xc[:, :, :], ALU.mult))
                then(dve.tensor_reduce(stat[0][:, :, :], sq[:, :, :], AX.X, ALU.add))
                dve.tensor_scalar(stat[2][:, :, :], stat[0][:, :, :], 1.0 / D, EPS, ALU.mult, ALU.add).then_inc(var_ready, 1)
                dve.wait_ge(std_ready, sqrt_no)
                then(dve.reciprocal(stat[4][:, :, :], stat[3][:, :, :]))
                then(dve.tensor_tensor(sq[:, :, :], xc[:, :, :], per_node(stat[4]), ALU.mult))
                dve.tensor_single_scalar(Hn[:, :, :], sq[:, :, :], 0.0, ALU.max).then_inc(h_ready, 1)

            def split():
                flat = pd[:, :, :].rearrange("p b d -> p (b d)")
                rest = pd_rest[:, :, :].rearrange("p b d -> p (b d)")
                then(dve.tensor_copy(attend_dst[:, 0, 0:NB * D], flat))
                then(dve.tensor_tensor(rest, flat, attend_dst[:, 0, 0:NB * D], ALU.subtract))
                then(dve.tensor_copy(attend_dst[:, 1, 0:NB * D], rest))
                dve.tensor_tensor(attend_dst[:, 2, 0:NB * D], rest, attend_dst[:, 1, 0:NB * D], ALU.subtract
                                  ).then_inc(pd_ready, 1)

            def onehot_rows(key, here, it, h):
                dve.wait_ge(here[h], (it + 1) * 16)
                dve.wait_ge(slot_free[key], it * 2 + h + 1)
                for w in range(2):
                    o = dve.tensor_scalar(onehot_t[h][:, w, :], local_ring[h][:, :], iota_part[:, w:w + 1], None,
                                          ALU.is_equal)
                o.then_inc(onehot_ready[key], 1)

            def count_block(it):
                K = 5
                dve.tensor_scalar(in_block, row_hi[:, :, :], iota_row[:, bass.ds(it, 1)], None, ALU.is_equal
                                  ).then_inc(rank_step, 1)
                dve.wait_ge(rank_step, it * K + 1)
                dve.tensor_tensor_scan(running.rearrange("p c e -> p (c e)"), keep_run.rearrange("p c e -> p (c e)"),
                                       in_block.rearrange("p c e -> p (c e)"), 0.0, ALU.mult, ALU.add
                                       ).then_inc(rank_step, 1)
                dve.wait_ge(rank_step, it * K + 2)
                dve.tensor_tensor(picked, in_block, running, ALU.mult).then_inc(rank_step, 1)
                dve.tensor_copy(tile_counts[:, :, bass.ds(it, 1)], running[:, :, P - 1:P]).then_inc(rank_step, 1)
                dve.wait_ge(rank_step, it * K + 4)
                dve.tensor_tensor(place, place, picked, ALU.add).then_inc(rank_step, 1)
                dve.wait_ge(rank_step, it * K + K)

            def place_block(it):
                dve.scalar_tensor_tensor(picked, row_hi[:, :, :], iota_row[:, bass.ds(it, 1)],
                                         place_base[:, :, bass.ds(it, 1)].to_broadcast([P, TC, P]),
                                         ALU.is_equal, ALU.mult).then_inc(place_step, 1)
                dve.wait_ge(place_step, it * 2 + 1)
                dve.tensor_tensor(place, place, picked, ALU.add).then_inc(place_step, 1)
                dve.wait_ge(place_step, it * 2 + 2)

            def sum_addresses(tile_block, tile_sum, tile_step, sums_at):
                for w in range(2):
                    then(dve.tensor_scalar(tile_sum[0:1, :], tile_block[0:1, :], float(w), float(W1), ALU.add, ALU.mult))
                    for j in range(1, ACC_BANKS):
                        then(dve.tensor_scalar(tile_step[0:1, :], tile_block[0:1, :], float(j * BPB - w),
                                               float(BANK - BPB * W1), ALU.is_ge, ALU.mult))
                        then(dve.tensor_tensor(tile_sum[0:1, :], tile_sum[0:1, :], tile_step[0:1, :], ALU.add))
                    then(dve.tensor_copy(sums_at[0:1, :, w], tile_sum[0:1, :]))

            def make_onehots(key, weight):
                with dve.Fori(0, IT) as it:
                    for h in range(2):
                        dve.wait_ge(slot_free[key], it * 2 + h + 1)
                        if key == "rel":
                            cols = bass.ds(it * (2 * H) + h * H, H)
                            dve.tensor_tensor(onehot_hi[h][:, :, :],
                                              iota_row[:, 0:NB].unsqueeze(1).to_broadcast([P, H, NB]),
                                              col_hi[:, cols].unsqueeze(2).to_broadcast([P, H, NB]),
                                              ALU.is_equal).then_inc(hi_ready, 1)
                        for u in range(H):
                            col = bass.ds(it * (2 * H) + (h * H + u), 1)
                            if weight is None:
                                o = dve.tensor_scalar(onehot[h][:, u, :], iota_row[:, :], col_local[:, col], None, ALU.is_equal)
                            else:
                                o = dve.tensor_scalar(onehot[h][:, u, :], iota_row[:, :], col_local[:, col], weight[:, col],
                                                      ALU.is_equal, ALU.mult)
                            if key == "rel":
                                dve.tensor_scalar(onehot_lo[h][:, u, :], iota_row[:, 0:P], col_lo[:, col], None, ALU.is_equal)
                        if key == "rel":
                            dve.wait_ge(hi_ready, it * 2 + h + 1)
                            o = dve.tensor_tensor(onehot_hi[h][:, :, :], onehot_hi[h][:, :, :],
                                                  col_weight[:, cols].unsqueeze(2).to_broadcast([P, H, NB]), ALU.mult)
                        o.then_inc(onehot_ready[key], 1)
                    if key == "ch0":
                        count_block(it)
                    if key == "ch1":
                        place_block(it)

            def take_sums(key):
                dve.wait_ge(slot_free[key], FREED)
                dve.tensor_copy(sums[:, :, :].rearrange("p (i b) c -> p i (b c)", i=ACC_BANKS),
                                acc[:, :].rearrange("p (i c) -> p i c", i=ACC_BANKS)[:, :, 0:BPB * W1]
                                ).then_inc(sums_taken[key], 1)
                dve.wait_ge(sums_taken[key], 1)

            S = sums[:, 0:NB, 0:D]
            count = sums[:, 0:NB, D:W1]

            dve.wait_ge(raw_loaded, RAW_LOADS * 16)
            then(dve.tensor_single_scalar(block_i[:, :, :], raw_dst[:, :, 0:1], P.bit_length() - 1, ALU.logical_shift_right))
            then(dve.tensor_copy(block_f[:, :, :], block_i[:, :, :]))
            then(dve.tensor_single_scalar(block_first[:, :, :], block_f[:, :, :], float(P), ALU.mult))
            then(dve.tensor_tensor(row_local[:, :, :], raw_dst[:, :, :], block_first[:, :, :].to_broadcast([P, TC, P]),
                                   ALU.subtract))
            dve.tensor_copy(local_bf[:, :, :], row_local[:, :, :]).then_inc(rows_derived, 1)
            dve.tensor_single_scalar(src_hi_i[:, :, :], raw_src[:, :, :], P.bit_length() - 1, ALU.logical_shift_right)
            then(dve.tensor_single_scalar(src_lo_i[:, :, :], raw_src[:, :, :], P - 1, ALU.bitwise_and))
            dve.tensor_copy(row_hi[:, :, :], src_hi_i[:, :, :])
            dve.tensor_copy(row_lo[:, :, :], src_lo_i[:, :, :])
            dve.tensor_copy(row_src[:, :, :], raw_src[:, :, :])
            dve.tensor_copy(ends[:, :, 0:1], raw_dst[:, :, 0:1])
            dve.tensor_copy(ends[:, :, 1:2], raw_dst[:, :, P - 1:P])
            same3 = same.rearrange("p (c e) -> p c e", c=TC)
            dve.memset(same3[:, :, 0:1], 0.0)
            dve.tensor_tensor(same3[:, :, 1:P], raw_dst[:, :, 1:P], raw_dst[:, :, 0:P - 1], ALU.is_equal)
            dve.scalar_tensor_tensor(row_rel[:, :, :], raw_src[:, :, :], float(R), raw_type[:, :, :], ALU.mult, ALU.add
                                     ).then_inc(rows_derived, 1)
            for i, c in enumerate((idx_src, idx_rel, col_local, col_hi, col_lo, col_weight)):
                dve.wait_ge(prep_turned, i + 1)
                dve.tensor_copy(c[:, :], work[i % 2][:, 0:T]).then_inc(prep_taken, 1)
            dve.wait_ge(tile_rows_turned, 3)
            then(dve.tensor_copy(tile_block[0:1, :], work[0][0:1, 0:T]))
            dve.tensor_copy(tile_ends[0:1, 0, :], work[1][0:1, 0:T])
            dve.tensor_copy(tile_ends[0:1, 1, :], work[2][0:1, 0:T])
            dve.tensor_single_scalar(pd_at[:, :], tile_block[0:1, :], float(D), ALU.mult)
            sum_addresses(tile_block, tile_sum, tile_step, sums_at)
            dve.tensor_tensor(whole[:, :], tile_ends[0:1, 0, :], tile_ends[0:1, 1, :], ALU.is_equal)
            dve.tensor_tensor(link[:, 1:T], tile_ends[0:1, 0, 1:T], tile_ends[0:1, 1, 0:T - 1], ALU.is_equal)
            dve.memset(link[:, 0:1], 0.0).then_inc(tile_info_ready, 1)
            dve.wait_ge(attn_w_turned, 1)
            dve.tensor_copy(w_attn_t[:, :, :].rearrange("d a j -> d (a j)"), work[3][0:D, 0:2 * D]).then_inc(attn_w_taken, 1)

            dve.wait_ge(x_loaded, 32)
            layernorm(0, 1)
            for b in range(NB):
                dve.wait_ge(mm_done[0], b + 1)
                dve.tensor_copy(relation_stage[:, b, :], work[2 + b % 2][:, 0:R * D]).then_inc(mm_taken[0], 1)
            make_onehots("rel", None)
            take_sums("rel")
            dve.tensor_copy(stat[5][:, :, :], work[0][:, 0:NB].unsqueeze(2))
            then(dve.tensor_single_scalar(stat[0][:, :, :], count, 1.0, ALU.max))
            then(dve.tensor_single_scalar(stat[1][:, :, :], count, 1.0, ALU.min))
            then(dve.reciprocal(stat[4][:, :, :], stat[0][:, :, :]))
            then(dve.tensor_tensor(xc[:, :, :], S, per_node(stat[4]), ALU.mult))
            then(dve.tensor_single_scalar(sq[:, :, :], xc[:, :, :], 1.0 - KEEP, ALU.mult))
            then(dve.scalar_tensor_tensor(xc[:, :, :], Hn[:, :, :], KEEP, sq[:, :, :], ALU.mult, ALU.add))
            then(dve.scalar_tensor_tensor(sq[:, :, :], xc[:, :, :], 0.0, Hn[:, :, :], ALU.max, ALU.subtract))
            then(dve.tensor_tensor(xc[:, :, :], sq[:, :, :], per_node(stat[1]), ALU.mult))
            then(dve.tensor_tensor(sq[:, :, :], xc[:, :, :], Hn[:, :, :], ALU.add))
            then(dve.tensor_tensor(X[:, :, :], X[:, :, :], sq[:, :, :], ALU.add))
            then(dve.tensor_single_scalar(stat[1][:, :, :], stat[5][:, :, :], 0.0, ALU.is_gt))
            then(dve.tensor_tensor(stat[0][:, :, :], stat[5][:, :, :], stat[1][:, :, :], ALU.mult))
            then(dve.tensor_scalar(stat[4][:, :, :], stat[1][:, :, :], -1.0, 1.0, ALU.mult, ALU.add))
            dve.tensor_tensor(stat[2][:, :, :], stat[0][:, :, :], stat[4][:, :, :], ALU.add).then_inc(var_ready, 1)
            dve.wait_ge(std_ready, 2)
            then(dve.reciprocal(stat[0][:, :, :], stat[3][:, :, :]))
            then(dve.tensor_tensor(dis[:, :, :], stat[0][:, :, :], stat[1][:, :, :], ALU.mult))
            then(dve.tensor_single_scalar(neg_dis[:, :, :], dis[:, :, :], -1.0, ALU.mult))

            if layers > 1:
                layernorm(1, 3)
                for g in range(NG):
                    bs = slice(g * GT, min((g + 1) * GT, NB))
                    n = bs.stop - bs.start
                    dve.wait_ge(mm_done[1], g + 1)
                    got = work[2 + g % 2][:, 0:n * 2 * D].rearrange("p (b a j) -> p b a j", b=n, a=2)
                    dve.tensor_copy(stage[:, bs, 0:D], got[:, :, 0, :])
                    dve.tensor_tensor(pd[:, bs, :], got[:, :, 1, :], b_attn[:, :].unsqueeze(1).to_broadcast([P, n, D]),
                                      ALU.add).then_inc(mm_taken[1], 1)
                dve.wait_ge(h_ready, 2)
                dve.tensor_copy(stage[:, :, D:2 * D], Hn[:, :, :]).then_inc(table_staged, 1)
                dve.wait_ge(mm_taken[1], NG)
                split()
                then(dve.scalar_tensor_tensor(w_abs[:, :], w_out[:, :], -1.0, w_out[:, :], ALU.mult, ALU.max))
                then(dve.tensor_reduce(above[:, :], w_abs[:, :], AX.X, ALU.add))
                then(dve.tensor_scalar(above[:, :], above[:, :], 1.0 + 2.0 ** -10, 1.0, ALU.mult, ALU.add))
                dve.memset(edge_rows[:, :, D:W1], 1.0).then_inc(prod_ready, 2)

                with dve.Fori(0, IT) as it:
                    for h in range(2):
                        onehot_rows("att", local_here, it, h)
                        dve.wait_ge(tanh_ready, it * 2 + h + 1)
                        dve.tensor_tensor(prod_ring[h][:, :, :], tanh_ring[h][:, :, :],
                                          w_out[:, :].unsqueeze(1).to_broadcast([P, H, D]), ALU.mult
                                          ).then_inc(prod_ready, 1)
                        dve.wait_ge(prod_ready, it * 2 + h + 3)
                        dve.tensor_reduce(score[:, bass.ds(it * (2 * H) + h * H, H)], prod_ring[h][:, :, :], AX.X, ALU.add
                                          ).then_inc(scores_ready, 1)
                dve.wait_ge(scores_ready, 2 * IT)
                dve.memset(V[:, TC - 1, :], 0.0)
                dve.tensor_scalar(shifted, score[:, :], above[:, 0:1], None, ALU.add).then_inc(shifted_ready, 1)
                dve.wait_ge(scores_turned, 1)
                dve.tensor_copy(V[:, 0:TC - 1, :], work[0][:, 0:(TC - 1) * P].rearrange("p (c e) -> p c e", c=TC - 1))
                then(dve.tensor_copy(V[0:TL, TC - 1, :], work[0][0:TL, (TC - 1) * P:TC * P]))

                def flat(a):
                    return a.rearrange("p c e -> p (c e)")

                def scans():
                    dve.tensor_tensor_scan(flat(prefix), same, flat(V), 0.0, ALU.mult, ALU.max)
                    return dve.tensor_tensor_scan(flat(suffix)[:, ::-1], same_next[:, ::-1], flat(V)[:, ::-1], 0.0,
                                                  ALU.mult, ALU.max)

                scans().then_inc(edge_vals_ready, 1)
                dve.memset(carry_f[0:1, :, :], 0.0)
                then(dve.memset(carry_b[0:1, :, :], 0.0))
                dve.tensor_tensor(carry_f[0:1, 0, 1:T], link[:, 1:T], whole[:, 0:T - 1], ALU.mult)
                dve.tensor_tensor(carry_b[0:1, 0, 0:T - 1], link[:, 1:T], whole[:, 1:T], ALU.mult)
                dve.wait_ge(edge_vals_turned, 1)
                dve.tensor_tensor(carry_f[0:1, 1, 1:T], link[:, 1:T], work[2][0:1, 0:T - 1], ALU.mult)
                then(dve.tensor_tensor(carry_b[0:1, 1, 0:T - 1], link[:, 1:T], work[3][0:1, 1:T], ALU.mult))
                dve.tensor_tensor_scan(carries[:, 0, :], carry_f[0:1, 0, :], carry_f[0:1, 1, :], 0.0, ALU.mult, ALU.max)
                dve.tensor_tensor_scan(carries[:, 1, :][:, ::-1], carry_b[0:1, 0, :][:, ::-1], carry_b[0:1, 1, :][:, ::-1],
                                       0.0, ALU.mult, ALU.max).then_inc(carries_ready, 1)
                dve.wait_ge(carries_turned, 1)
                dve.tensor_copy(carry_cols[:, :, 0:TC - 1], work[1][:, 0:2 * TC].rearrange("p (i c) -> p i c", i=2)[:, :, 0:TC - 1])
                then(dve.tensor_copy(carry_cols[0:TL, :, TC - 1:TC],
                                     work[1][0:TL, 0:2 * TC].rearrange("p (i c) -> p i c", i=2)[:, :, TC - 1:TC]))
                for i, e in enumerate((0, P - 1)):
                    for rows_, cs in ((P, slice(0, TC - 1)), (TL, slice(TC - 1, TC))):
                        then(dve.tensor_tensor(V[0:rows_, cs, e], V[0:rows_, cs, e], carry_cols[0:rows_, i, cs], ALU.max))
                then(scans())
                dve.tensor_tensor(flat(prefix), flat(prefix), flat(suffix), ALU.max).then_inc(max_ready, 1)
                dve.wait_ge(max_turned, 1)
                then(dve.tensor_scalar(shift, work[2][:, 0:T], above[:, 0:1], None, ALU.subtract))
                dve.tensor_tensor(expo, score[:, :], shift, ALU.subtract).then_inc(expo_ready, 1)
                dve.wait_ge(weight_ready, 1)
                make_onehots("agg", weight_e)
                take_sums("agg")
                then(dve.tensor_single_scalar(stat[0][:, :, :], count, 0.0, ALU.is_equal))
                then(dve.tensor_tensor(stat[1][:, :, :], stat[0][:, :, :], count, ALU.add))
                then(dve.reciprocal(stat[4][:, :, :], stat[1][:, :, :]))
                then(dve.tensor_tensor(xc, S, per_node(stat[4]), ALU.mult))
                then(dve.tensor_tensor(X[:, :, :], X[:, :, :], xc, ALU.add))

            if layers > 2:
                layernorm(2, 4)
                dve.wait_ge(h_ready, 3)
                dve.tensor_tensor(stage[:, :, 0:D], Hn[:, :, :], per_node(dis), ALU.mult).then_inc(table_staged, 1)
                then(dve.tensor_tensor(bias_cheb[:, :, :], b_cheb[:, 0, :, :], b_cheb[:, 1, :, :], ALU.add))
                dve.memset(keep_run[:, :, 1:P], 1.0)
                dve.memset(keep_run[:, :, 0:1], 0.0)
                then(dve.memset(place, 0.0))
                make_onehots("ch0", col_weight)
                then(dve.memset(place_base, 0.0))
                dve.wait_ge(rank_step, IT * 5)
                dve.memset(block_total, 1.0).then_inc(tile_counts_ready, 1)
                take_sums("ch0")
                dve.tensor_tensor(Tx1[:, :, :], S, per_node(neg_dis), ALU.mult).then_inc(h_ready, 1)
                dve.wait_ge(h_ready, 4)
                dve.tensor_tensor(stage[:, :, 0:D], Tx1[:, :, :], per_node(dis), ALU.mult).then_inc(table_staged, 1)
                dve.wait_ge(bases_ready, 1)
                then(dve.tensor_copy(block_start, work[3][:, 0:NB + 1]))
                then(dve.tensor_tensor_scan(block_total, ones[:, 0:NB + 1], block_start, 0.0, ALU.mult, ALU.add))
                then(dve.tensor_tensor(block_start, block_total, block_start, ALU.subtract))
                then(dve.tensor_tensor(place_base, work[2][:, 0:TC * (NB + 1)].rearrange("p (c b) -> p c b", c=TC),
                                       block_start.unsqueeze(1).to_broadcast([P, TC, NB + 1]), ALU.add))
                make_onehots("ch1", col_weight)
                dve.wait_ge(place_step, IT * 2)
                then(dve.tensor_single_scalar(place, place, 1.0, ALU.subtract))
                for c in range(TC):
                    dve.tensor_scalar(sorted_first[:, c, :], iota_part[:, 0:1], float(P), float(c * P * P), ALU.mult, ALU.add)
                then(dve.memset(sorted_block, 0.0))
                then(dve.tensor_tensor(starts_here, block_start.unsqueeze(1).to_broadcast([P, TC, NB + 1]),
                                       sorted_first.to_broadcast([P, TC, NB + 1]), ALU.is_le))
                then(dve.tensor_reduce(sorted_block, starts_here, AX.X, ALU.add))
                dve.tensor_single_scalar(sorted_block, sorted_block, 1.0, ALU.subtract).then_inc(places_ready, 1)
                dve.wait_ge(places_turned, 1)
                dve.tensor_copy(idx_place, work[2][:, 0:T]).then_inc(places_ready, 1)
                then(dve.tensor_copy(sorted_base[0:1, :], work[3][0:1, 0:T]))
                dve.tensor_single_scalar(sorted_row[0:1, :], sorted_base[0:1, :], float(P), ALU.mult).then_inc(places_ready, 1)
                sum_addresses(sorted_base, sorted_sum, sorted_step, sorted_at)
                dve.memset(sorted_step[0:1, :], 0.0).then_inc(places_ready, 1)
                dve.wait_ge(places_turned, 2)
                dve.tensor_copy(sorted_base, work[2][:, 0:T]).then_inc(places_ready, 1)
                take_sums("ch1")
                then(dve.tensor_single_scalar(stat[0][:, :, :], neg_dis[:, :, :], 2.0, ALU.mult))
                then(dve.tensor_tensor(sq, S, per_node(stat[0]), ALU.mult))
                dve.tensor_tensor(Tx2[:, :, :], sq, Hn[:, :, :], ALU.subtract).then_inc(h_ready, 1)
                for g in range(NG):
                    bs = slice(g * GT, min((g + 1) * GT, NB))
                    n = bs.stop - bs.start
                    dve.wait_ge(mm_done[2], g + 1)
                    o = dve.tensor_tensor(stage[:, bs, :], work[2 + g % 2][:, 0:n * 2 * D].rearrange("p (b c) -> p b c", b=n),
                                          bias_cheb[:, :, :].rearrange("p a d -> p (a d)").unsqueeze(1)
                                          .to_broadcast([P, n, 2 * D]), ALU.add)
                    o.then_inc(mm_taken[2], 1)
                dve.wait_ge(mm_taken[2], NG)
                dve.memset(stat[5][:, :, :], 0.0).then_inc(gates_ready, 1)
                dve.wait_ge(gates_done, 2)
                then(dve.tensor_tensor(xc, Tx1[:, :, :], Tx2[:, :, :], ALU.mult))
                then(dve.tensor_tensor(X[:, :, :], X[:, :, :], xc, ALU.add))

            if layers > 3:
                layernorm(3, 5)
                for g in range(NG):
                    bs = slice(g * GT, min((g + 1) * GT, NB))
                    n = bs.stop - bs.start
                    dve.wait_ge(mm_done[3], g + 1)
                    dve.tensor_copy(pd[:, bs, :], work[2 + g % 2][:, 0:n * D].rearrange("p (b c) -> p b c", b=n)
                                    ).then_inc(mm_taken[3], 1)
                dve.wait_ge(mm_taken[3], NG)
                split()
                dve.tensor_tensor(X[:, :, :], X[:, :, :], b_gcn[:, :].unsqueeze(1).to_broadcast([P, NB, D]), ALU.add
                                  ).then_inc(msgs_ready, 2)
                def message_step(it, first):
                    for h in range(2):
                        onehot_rows("msg", local_here3, it, h)
                        if not first:
                            dve.wait_ge(scattered[h], it * (16 * H))
                        cols = bass.ds(it * (2 * H) + h * H, H)
                        dve.tensor_copy(rows[h][:, :, D:W1], idx_src[:, cols].unsqueeze(2))
                        dve.wait_ge(slot_free["msg"], it * 2 + h + 3)
                        dve.tensor_tensor(rows[h][:, :, 0:D], work[2 + h][:, :].rearrange("p (t d) -> p t d", t=H),
                                          col_weight[:, cols].unsqueeze(2).to_broadcast([P, H, D]), ALU.mult
                                          ).then_inc(msgs_ready, 1)

                message_step(0, True)
                with dve.Fori(1, IT) as it:
                    message_step(it, False)
                with dve.Fori(0, IT) as it:
                    for h in range(2):
                        dve.wait_ge(slot_free["gcn"], it * 2 + h + 1)
                        dve.wait_ge(sorted_here[h], (it + 1) * 16)
                        dve.tensor_tensor(local_src[h][:, :, :], rows[h][:, :, D:W1],
                                          sorted_base[:, bass.ds(it * (2 * H) + h * H, H)].unsqueeze(2), ALU.subtract
                                          ).then_inc(local_src_ready, 1)
                        dve.wait_ge(local_src_ready, it * 2 + h + 1)
                        for u in range(H):
                            o = dve.tensor_scalar(onehot[h][:, u, :], iota_row[:, :], local_src[h][:, u, :], None, ALU.is_equal)
                        o.then_inc(onehot_ready["gcn"], 1)
                take_sums("gcn")
                then(dve.tensor_tensor(X[:, :, :], X[:, :, :], S, ALU.add))
            dve.memset(stat[5][:, :, :], 0.0).then_inc(out_ready, 1)

        return nc


_INS = ["x", "src", "dst", "edge_type_8", "edge_weight", "L0_gnn_weight_r", "L1_gnn_W_attn", "L1_gnn_b_attn",
        "L1_gnn_w_out", "L2_gnn_Wxz", "L2_gnn_bxz", "L2_gnn_bhz", "L2_gnn_Wxh", "L2_gnn_bxh", "L2_gnn_bhh",
        "L3_gnn_weight", "L3_gnn_bias"]


def kernel(**inputs):
    import numpy as np
    import concourse.bacc as bacc
    from concourse.bass_utils import run_bass_kernel_spmd

    nc = bacc.Bacc("TRN2", target_bir_lowering=False, num_devices=1)
    arrays = {f"in_{n}": np.ascontiguousarray(inputs[n]) for n in _INS}
    aps = {n: nc.dram_tensor(f"in_{n}", arrays[f"in_{n}"].shape, mybir.dt.from_np(arrays[f"in_{n}"].dtype),
                             kind="ExternalInput").ap() for n in _INS}
    shape = inputs["x"].shape
    out = nc.dram_tensor("out_x", shape, F32, kind="ExternalOutput").ap()
    gnn_kernel(nc, aps, out)
    r = run_bass_kernel_spmd(nc, [arrays], core_ids=[0])
    return r.results[0]["out_x"]
```

```python
from contextlib import ExitStack

import concourse.bass as bass
from concourse import mybir
from concourse.alu_op_type import AluOpType as ALU

F32, I32, BF16, I16 = mybir.dt.float32, mybir.dt.int32, mybir.dt.bfloat16, mybir.dt.int16
ACT = mybir.ActivationFunctionType
AX = mybir.AxisListType
PE_ENGINE = mybir.EngineType.PE


def gnn_kernel(nc, ins, out, layers=4):
    P = 128
    N, D = ins["x"].shape
    E = ins["src"].shape[0]
    R = ins["L0_gnn_weight_r"].shape[0]
    NB = -(-N // P)
    NFULL = N // P
    NREST = N - NFULL * P
    T = -(-E // P)
    H = 8
    IT = T // (2 * H)
    assert IT * 2 * H == T and N < NB * P
    TC = -(-T // P)
    TL = T - (TC - 1) * P
    EFULL = E // P
    EREST = E - EFULL * P
    BANK = 512
    ACC_BANKS = -(-(NB + 1) * D // BANK)
    COUNTS = ACC_BANKS * BANK - 4 * (NB + 1)
    assert COUNTS >= (NB + 1) * D
    EPS = 1e-5
    KEEP = 0.2
    GT = 4
    NG = -(-NB // GT)

    ctx = ExitStack()
    with ctx:
        def sb(name, shape, dt=F32):
            return ctx.enter_context(nc.sbuf_tensor(name, shape, dt))

        def ps(name, shape, dt=F32):
            return ctx.enter_context(nc.psum_tensor(name, shape, dt))

        def sem(name):
            return ctx.enter_context(nc.semaphore(name))

        relation_rows = nc.dram_tensor("relation_rows", [NB * P, R * D], F32).ap()
        attention_rows = nc.dram_tensor("attention_rows", [NB * P, 2 * D], F32).ap()
        cheb_rows = [nc.dram_tensor(f"cheb_rows{i}", [NB * P, D], F32).ap() for i in range(2)]
        support_rows = nc.dram_tensor("support_rows", [NB * P, D], F32).ap()
        sorted_edges = nc.dram_tensor("sorted_edges", [T * P, 3], F32).ap()
        source_rows = {k: nc.dram_tensor(f"source_rows_{k}", [TC * P, P], I16).ap() for k in ("src", "dst")}
        local_rows = nc.dram_tensor("local_rows", [TC * P, P], BF16).ap()

        def carve(mem, at, shape, dt=F32):
            n = 1
            for x in shape:
                n *= x
            words = n // 2 if dt in (BF16, I16) else n
            view = mem[:, at:at + words]
            view = view if dt == F32 else view.bitcast(dt)
            if len(shape) == 2:
                view = view.rearrange("p (a b) -> p a b", a=shape[0])
            return view, at + words

        big = sb("big", [P, T * D])
        edge_rows = big[:, :].rearrange("p (t c) -> p t c", t=T)
        relation_stage, at = carve(big, 0, [NB, R * D])
        _, at = carve(big, at, [NB * P])
        raw_dst, at = carve(big, at, [TC, P], I32)
        raw_src, at = carve(big, at, [TC, P], I32)
        raw_type, at = carve(big, at, [TC, P], I32)
        raw_weight, at = carve(big, at, [TC, P])
        src_hi_i, at = carve(big, at, [TC, P], I32)
        src_lo_i, at = carve(big, at, [TC, P], I32)
        row_vals = []
        for _ in range(4):
            view, at = carve(big, at, [TC, P])
            row_vals.append(view)
        row_src, row_rel, row_local, row_lo = row_vals
        local_bf, at = carve(big, at, [TC, P], BF16)
        src_i16, at = carve(big, at, [TC, P], I16)
        idx_rel, at = carve(big, at, [T], I32)
        col_hi, at = carve(big, at, [T])
        col_lo, at = carve(big, at, [T])
        tile_block, at = carve(big, at, [T])
        tile_ends, at = carve(big, at, [2, T])
        degree_parts, at = carve(big, at, [T, 3], BF16)
        degree_rest, at = carve(big, at, [T, 1])
        w_rel, at = carve(big, at, [R, D])
        w_rel = w_rel[0:D]
        assert at <= T * D
        pd, _ = carve(big, 0, [NB, D])
        pd_rest, _ = carve(big, NB * D, [NB, D])
        Tx1, _ = carve(big, 0, [NB, D])
        Tx2, _ = carve(big, NB * D, [NB, D])
        hT = []
        for i in range(3):
            view, _ = carve(big, NB * R * D, [NB * P]) if i == 0 else carve(big, (2 * D + (i - 1) * P) * NB, [NB * P])
            hT.append(view[0:D, :])
        assert (2 * D + 2 * P) * NB <= NB * R * D
        at = NB * (R * D + P)
        keep_run, at = carve(big, at, [TC, P])
        in_block, at = carve(big, at, [TC, P])
        running, at = carve(big, at, [TC, P])
        at = NB * (R * D + P)
        sorted_rows, at = carve(big, at, [TC, 3 * P])
        row_local_src, at = carve(big, at, [TC, P])
        row_dst_sorted, at = carve(big, at, [TC, P])
        row_weight_sorted, at = carve(big, at, [TC, P])
        idx_dst, at = carve(big, at, [T], I32)
        col_local_src, at = carve(big, at, [T])
        col_weight_sorted, at = carve(big, at, [T])
        dst_i16, at = carve(big, at, [TC, P], I16)
        table_parts, at = carve(big, at, [NB, 3 * D], BF16)
        wanted, at = carve(big, at, [2, P], I16)
        onehot_src, _ = carve(big, 2 * (D + P) * NB, [NB, 2 * P], BF16)
        assert 2 * (D + P) * NB + NB * P <= NB * R * D
        assert at <= T * D and IT > NB

        idx_src = sb("idx_src", [P, T], I32)
        col_local = sb("col_local", [P, T])
        col_weight = sb("col_weight", [P, T])
        score = sb("score", [P, T])
        row_hi = sb("row_hi", [P, TC, P])
        place = sb("place", [P, TC, P])
        tile_counts = sb("tile_counts", [P, TC, NB + 1])
        place_base = sb("place_base", [P, TC, NB + 1])
        starts_here = sb("starts_here", [P, TC, NB + 1])
        block_total = sb("block_total", [P, NB + 1])
        block_start = sb("block_start", [P, NB + 1])
        sorted_first = sb("sorted_first", [P, TC, 1])
        sorted_block = sb("sorted_block", [P, TC, 1])
        weight_e = score
        same_flags = sb("same_flags", [P, TC * P + 1])
        same = same_flags[:, 0:TC * P]
        same_next = same_flags[:, 1:TC * P + 1]
        block_i = sb("block_i", [P, TC, 1], I32)
        block_f = sb("block_f", [P, TC, 1])
        block_first = sb("block_first", [P, TC, 1])
        ends = sb("ends", [P, TC, 2])
        block_at = sb("block_at", [1, T], I32)
        whole = sb("whole", [1, T])
        link = sb("link", [1, T])
        ident = sb("ident", [P, P])
        iota_wide, _ = carve(big, 0, [2 * P])
        iota_row = sb("iota_row", [P, NB + 1])
        iota_bf = sb("iota_bf", [P, 2 * P], BF16)
        ones_bf = sb("ones_bf", [P, 1], BF16)
        iota_part = sb("iota_part", [P, NB])
        zeros = sb("zeros", [P, BANK], BF16)
        before = sb("before", [P, P])
        ones = sb("ones", [P, P])
        w_attn = sb("w_attn", [D, 2 * D])
        w_attn_t = sb("w_attn_t", [D, 2, D])
        b_attn = sb("b_attn", [P, D])
        w_out = sb("w_out", [P, D])
        w_cheb = sb("w_cheb", [D, 3, 2, D])
        b_cheb = sb("b_cheb", [P, 2, 2, D])
        bias_cheb = sb("bias_cheb", [P, 2, D])
        w_gcn = sb("w_gcn", [D, D])
        b_gcn = sb("b_gcn", [P, D])
        X = sb("X", [P, NB, D])
        Hn = sb("Hn", [P, NB, D])
        stat = [sb(f"stat{i}", [P, NB, 1]) for i in range(6)]
        dis = sb("dis", [P, NB, 1])
        neg_dis = sb("neg_dis", [P, NB, 1])
        stage_mem = sb("stage_mem", [P, NB * 2 * D])
        stage = stage_mem[:, :].rearrange("p (b c) -> p b c", b=NB)
        xc, at = carve(stage_mem, 0, [NB, D])
        sq, _ = carve(stage_mem, at, [NB, D])
        picked, _ = carve(stage_mem, 0, [TC, P])
        shifted, at = carve(stage_mem, 0, [T])
        shift, at = carve(stage_mem, at, [T])
        expo, at = carve(stage_mem, at, [T])
        carry_f, at = carve(stage_mem, at, [2, T])
        carry_b, at = carve(stage_mem, at, [2, T])
        count_parts, _ = carve(stage_mem, 3 * T, [T, 3], BF16)
        weight_rest, _ = carve(stage_mem, 5 * T, [T, 1])
        assert at <= NB * 2 * D
        carries = sb("carries", [1, 2, T])
        carry_cols = sb("carry_cols", [P, 2, TC])
        idx_ring = [sb(f"idx_ring{h}", [P, H], I32) for h in range(2)]
        row_ring = [sb(f"row_ring{h}", [P, H * 2 * D]) for h in range(2)]
        rows2 = [carve(row_ring[h], 0, [H, 2 * D])[0] for h in range(2)]
        rows = [carve(row_ring[h], 0, [H, D])[0] for h in range(2)]
        msg = [sb(f"msg{h}", [P, H, D]) for h in range(2)]
        rest = [sb(f"rest{h}", [P, H, D]) for h in range(2)]
        part_ring = [sb(f"part_ring{h}", [P, H * 3 * D // 2]) for h in range(2)]
        parts = [carve(part_ring[h], 0, [H, 3 * D], BF16)[0] for h in range(2)]
        place_ring = [sb(f"place_ring{h}", [P, H], I32) for h in range(2)]
        record_ring = [sb(f"record_ring{h}", [P, H, 3]) for h in range(2)]
        hot_ring = [sb(f"hot_ring{h}", [P, H * (P + P // 2 + 2 * NB)]) for h in range(2)]
        onehot, onehot_lo, onehot_hi, hi_parts = [], [], [], []
        onehot_t, local_ring = [], []
        for h in range(2):
            at = 0
            for kept, shape in ((onehot, [H, 2 * P]), (onehot_lo, [H, P]), (onehot_hi, [H, NB]), (hi_parts, [H, 3 * NB])):
                view, at = carve(hot_ring[h], at, shape, BF16)
                kept.append(view)
            view, at = carve(hot_ring[h], 0, [H * P], BF16)
            local_ring.append(view)
            view, at = carve(hot_ring[h], at, [2, H * P], BF16)
            onehot_t.append(view)
        V, at = carve(hot_ring[0], 0, [TC, P])
        prefix, at = carve(hot_ring[0], at, [TC, P])
        suffix, at = carve(hot_ring[1], 0, [TC, P])
        attend_mem = sb("attend_mem", [P, (NB + 1) * 3 * D // 2])
        attend_dst, _ = carve(attend_mem, 0, [NB + 1, 3 * D], BF16)
        records, at = carve(attend_mem, 0, [T, 3])
        idx_place, at = carve(attend_mem, at, [T], I32)
        tile_base, at = carve(attend_mem, at, [T])
        sorted_block_at, at = carve(attend_mem, at, [T], I32)
        assert at <= (NB + 1) * 3 * D // 2
        above = sb("above", [P, 1])

        acc = ps("acc", [P, ACC_BANKS * BANK])
        work = [ps(f"work{i}", [P, BANK]) for i in range(4)]

        raw_cleared = sem("raw_cleared")
        x_cleared = sem("x_cleared")
        consts_ready = sem("consts_ready")
        raw_loaded = sem("raw_loaded")
        x_loaded = sem("x_loaded")
        params_loaded = sem("params_loaded")
        rows_derived = sem("rows_derived")
        local_stored = sem("local_stored")
        prep_turned = sem("prep_turned")
        prep_taken = sem("prep_taken")
        tile_rows_turned = sem("tile_rows_turned")
        tile_info_ready = sem("tile_info_ready")
        attn_w_turned = sem("attn_w_turned")
        attn_w_taken = sem("attn_w_taken")
        var_ready = sem("var_ready")
        std_ready = sem("std_ready")
        h_ready = sem("h_ready")
        turned = sem("turned")
        turn_taken = sem("turn_taken")
        mm_done = [sem(f"mm_done{k}") for k in range(4)]
        mm_taken = [sem(f"mm_taken{k}") for k in range(4)]
        table_staged = sem("table_staged")
        passes = ["rel", "att", "ch0", "ch1", "gcn"]
        table_stored = {k: sem(f"table_stored_{k}") for k in passes}
        idx_copied = {k: sem(f"idx_copied_{k}") for k in passes}
        gathered = {k: [sem(f"gathered_{k}{h}") for h in range(2)] for k in passes}
        FREED = 2 * IT + 2
        sum_passes = ["rel", "agg", "ch0", "ch1", "gcn"]
        slot_free = {k: sem(f"slot_free_{k}") for k in [*sum_passes, "att"]}
        onehot_ready = {k: sem(f"onehot_ready_{k}") for k in [*sum_passes, "att"]}
        msg_ready = {k: sem(f"msg_ready_{k}") for k in sum_passes}
        part1_ready = {k: sem(f"part1_ready_{k}") for k in sum_passes}
        rest_ready = {k: sem(f"rest_ready_{k}") for k in sum_passes}
        part2_ready = {k: sem(f"part2_ready_{k}") for k in sum_passes}
        rows_free = {k: sem(f"rows_free_{k}") for k in passes}
        sums_taken = {k: sem(f"sums_taken_{k}") for k in sum_passes}
        rank_step = sem("rank_step")
        place_step = sem("place_step")
        tile_counts_ready = sem("tile_counts_ready")
        bases_ready = sem("bases_ready")
        places_ready = sem("places_ready")
        places_turned = sem("places_turned")
        bases_taken = sem("bases_taken")
        HYBRID = ("ch0", "ch1", "gcn")
        wanted_here = {k: sem(f"wanted_here_{k}") for k in HYBRID}
        src_onehot_ready = {k: sem(f"src_onehot_ready_{k}") for k in HYBRID}
        found_ready = {k: sem(f"found_ready_{k}") for k in HYBRID}
        found_read = {k: sem(f"found_read_{k}") for k in HYBRID}
        source_rows_stored = {k: sem(f"source_rows_stored_{k}") for k in ("src", "dst")}
        records_ready = sem("records_ready")
        records_copied = sem("records_copied")
        scattered = [sem(f"scattered{h}") for h in range(2)]
        sorted_loaded = sem("sorted_loaded")
        sorted_rows_ready = sem("sorted_rows_ready")
        sorted_turned = sem("sorted_turned")
        sorted_taken = sem("sorted_taken")
        local_here = [sem(f"local_here{h}") for h in range(2)]
        pd_ready = sem("pd_ready")
        bank_read = sem("bank_read")
        tanh_ready = sem("tanh_ready")
        rows_kept = sem("rows_kept")
        prod_ready = sem("prod_ready")
        hi_ready = sem("hi_ready")
        scores_ready = sem("scores_ready")
        shifted_ready = sem("shifted_ready")
        scores_turned = sem("scores_turned")
        edge_vals_ready = sem("edge_vals_ready")
        edge_vals_turned = sem("edge_vals_turned")
        carries_ready = sem("carries_ready")
        carries_turned = sem("carries_turned")
        max_ready = sem("max_ready")
        max_turned = sem("max_turned")
        expo_ready = sem("expo_ready")
        weight_ready = sem("weight_ready")
        gates_ready = sem("gates_ready")
        gates_done = sem("gates_done")
        vec = sem("vec")
        out_ready = sem("out_ready")
        out_stored = sem("out_stored")

        RAW_LOADS = 4 * 3
        SCATTER_STEPS = (21, 22)
        CONSTS = 12
        block = ctx.enter_context(nc.Block())

        def by_pool(key):
            return H - 1 if key in HYBRID else H

        def blocks_of(table):
            return table.rearrange("(b p) c -> p b c", p=P)

        @block.sync
        def _(sp):
            def broadcast_local(key, here):
                with sp.Fori(0, IT) as it:
                    for h in range(2):
                        sp.wait_ge(slot_free[key], it * 2 + h + 1)
                        sp.dma_start(local_ring[h][:, :],
                                     local_rows[bass.ds(it * (2 * H) + h * H, H), :].rearrange("(a t) p -> a (t p)", a=1)
                                     .to_broadcast([P, H * P])).then_inc(here[h], 16)

            def broadcast_wanted(key, which, stores):
                def step(it, first):
                    if not first:
                        sp.wait_ge(src_onehot_ready[key], it)
                    sp.dma_start(wanted[:, :, :],
                                 source_rows[which][bass.ds(it * (2 * H), 2 * H), :]
                                 .rearrange("(x a u) p -> x a u p", x=1, u=H)[:, :, H - 1, :].to_broadcast([P, 2, P])
                                 ).then_inc(wanted_here[key], 16)

                sp.wait_ge(source_rows_stored[which], 16 * stores)
                step(0, True)
                with sp.Fori(1, IT) as it:
                    step(it, False)

            fulls = (TC - 1) * P
            pairs = ((raw_dst, "dst"), (raw_src, "src"), (raw_type, "edge_type_8"), (raw_weight, "edge_weight"))
            for tile, name in pairs:
                sp.dma_start(tile[:, 0:TC - 1, :], ins[name][0:fulls * P].rearrange("(c t p) -> t c p", t=P, p=P)
                             ).then_inc(raw_loaded, 16)
            sp.wait_ge(raw_cleared, 4)
            for tile, name in pairs:
                sp.dma_start(tile[0:EFULL - fulls, TC - 1, :],
                             ins[name][fulls * P:EFULL * P].rearrange("(t p) -> t p", p=P)).then_inc(raw_loaded, 16)
                sp.dma_start(tile[EFULL - fulls:EFULL - fulls + 1, TC - 1, 0:EREST],
                             ins[name][EFULL * P:E].rearrange("(t p) -> t p", t=1)).then_inc(raw_loaded, 16)
            sp.dma_start(X[:, 0:NFULL, :], ins["x"][0:NFULL * P, :].rearrange("(b p) d -> p b d", p=P)
                         ).then_inc(x_loaded, 16)
            sp.wait_ge(x_cleared, 1)
            sp.dma_start(X[0:NREST, NFULL, :], ins["x"][NFULL * P:N, :]).then_inc(x_loaded, 16)
            sp.dma_start(w_rel[:, :, :], ins["L0_gnn_weight_r"].rearrange("r d f -> d r f")).then_inc(params_loaded, 16)
            sp.dma_start(w_attn[:, :], ins["L1_gnn_W_attn"]).then_inc(params_loaded, 16)
            for k in range(3):
                for g, name in enumerate(("L2_gnn_Wxz", "L2_gnn_Wxh")):
                    sp.dma_start(w_cheb[:, k, g, :], ins[name][k, :, :]).then_inc(params_loaded, 16)
            sp.dma_start(w_gcn[:, :], ins["L3_gnn_weight"]).then_inc(params_loaded, 16)
            vectors = [(b_attn[:, :], "L1_gnn_b_attn"), (w_out[:, :], "L1_gnn_w_out"), (b_gcn[:, :], "L3_gnn_bias")]
            vectors += [(b_cheb[:, i // 2, i % 2, :], "L2_gnn_" + n) for i, n in enumerate(("bxz", "bxh", "bhz", "bhh"))]
            for tile, name in vectors:
                sp.dma_start(tile, ins[name].rearrange("(a d) -> a d", a=1).to_broadcast([P, D])
                             ).then_inc(params_loaded, 16)
            sp.wait_ge(rows_derived, 1)
            sp.dma_start(local_rows.rearrange("(c t) p -> t c p", t=P), local_bf[:, :, :]).then_inc(local_stored, 16)
            sp.wait_ge(rows_derived, 2)
            sp.dma_start(source_rows["src"].rearrange("(c t) p -> t c p", t=P), src_i16
                         ).then_inc(source_rows_stored["src"], 16)

            for j in range(5):
                s = slice(j * NB // 5, (j + 1) * NB // 5)
                sp.wait_ge(mm_taken[0], s.stop)
                sp.dma_start(blocks_of(relation_rows)[:, s, :], relation_stage[:, s, :]).then_inc(table_stored["rel"], 16)

            if layers > 1:
                sp.wait_ge(table_staged, 1)
                sp.dma_start(blocks_of(attention_rows), stage[:, :, :]).then_inc(table_stored["att"], 16)
                sp.wait_ge(local_stored, 16)
                broadcast_local("att", local_here)
            for i, k in enumerate(("ch0", "ch1")):
                if layers > 2:
                    sp.wait_ge(table_staged, 2 + i)
                    sp.dma_start(blocks_of(cheb_rows[i]), stage[:, :, 0:D]).then_inc(table_stored[k], 16)
                    broadcast_wanted(k, "src", 1)
            if layers > 3:
                sp.wait_ge(table_staged, 4)
                sp.dma_start(blocks_of(support_rows), stage[:, :, 0:D]).then_inc(table_stored["gcn"], 16)
                for h in range(2):
                    sp.wait_ge(scattered[h], IT * 16 * H)
                fulls = (TC - 1) * P
                sp.dma_start(sorted_rows[:, 0:TC - 1, :], sorted_edges[0:fulls * P, :]
                             .rearrange("(c t e) j -> t c (e j)", t=P, e=P)).then_inc(sorted_loaded, 16)
                sp.dma_start(sorted_rows[0:TL, TC - 1, :], sorted_edges[fulls * P:, :]
                             .rearrange("(t e) j -> t (e j)", e=P)).then_inc(sorted_loaded, 16)
                sp.wait_ge(sorted_rows_ready, 1)
                sp.dma_start(source_rows["dst"][0:fulls, :].rearrange("(c t) p -> t c p", t=P), dst_i16[:, 0:TC - 1, :]
                             ).then_inc(source_rows_stored["dst"], 16)
                sp.dma_start(source_rows["dst"][fulls:fulls + TL, :], dst_i16[0:TL, TC - 1, :]
                             ).then_inc(source_rows_stored["dst"], 16)
                broadcast_wanted("gcn", "dst", 2)
            sp.wait_ge(out_ready, 1)
            sp.dma_start(out[0:NFULL * P, :].rearrange("(b p) d -> p b d", p=P), X[:, 0:NFULL, :]).then_inc(out_stored, 16)
            sp.dma_start(out[NFULL * P:N, :], X[0:NREST, NFULL, :]).then_inc(out_stored, 16)
            sp.wait_ge(out_stored, 32)

        @block.gpsimd
        def _(pool):
            last = TC - 1
            pool.memset(raw_dst[:, last, :], 1 << 14).then_inc(raw_cleared, 1)
            pool.memset(raw_src[:, last, :], NB * P - 1).then_inc(raw_cleared, 1)
            pool.memset(raw_type[:, last, :], 0).then_inc(raw_cleared, 1)
            pool.memset(raw_weight[:, last, :], 0.0).then_inc(raw_cleared, 1)
            pool.memset(X[:, NFULL, :], 0.0).then_inc(x_cleared, 1)
            pool.memset(ident[:, :], 0.0).then_inc(consts_ready, 1)
            pool.iota(iota_wide, [[1, 2 * P]], base=0, channel_multiplier=0,
                      allow_small_or_imprecise_dtypes=True).then_inc(consts_ready, 1)
            pool.iota(iota_part[:, :], [[P, NB]], base=0, channel_multiplier=1,
                      allow_small_or_imprecise_dtypes=True).then_inc(consts_ready, 1)
            pool.memset(zeros[:, :], 0.0).then_inc(consts_ready, 1)
            pool.wait_ge(consts_ready, 4)
            pool.affine_select(out=ident[:, :], in_=ident[:, :], compare_op=ALU.not_equal, fill=1.0,
                               base=0, pattern=[[-1, P]], channel_multiplier=1).then_inc(consts_ready, 1)
            pool.memset(ones[:, :], 1.0).then_inc(consts_ready, 1)
            pool.memset(ones_bf[:, :], 1.0).then_inc(consts_ready, 1)
            pool.wait_ge(consts_ready, 7)
            pool.affine_select(out=before[:, :], in_=ones[:, :], compare_op=ALU.is_gt, fill=0.0,
                               base=0, pattern=[[1, P]], channel_multiplier=-1).then_inc(consts_ready, 1)
            pool.tensor_copy(iota_row[:, :], iota_wide[:, 0:NB + 1]).then_inc(consts_ready, 1)
            pool.tensor_copy(iota_bf[:, :], iota_wide).then_inc(consts_ready, 1)
            pool.memset(attend_dst[:, NB, :], 0.0).then_inc(consts_ready, 1)
            pool.memset(same_flags[:, TC * P:TC * P + 1], 0.0).then_inc(consts_ready, 1)

            def gather(key, table, ring, width, stores):
                pool.wait_ge(table_stored[key], 16 * stores)
                with pool.Fori(0, IT) as it:
                    for h in range(2):
                        pool.wait_ge(rows_free[key], it * 2 + h + 1)
                        pool.wait_ge(idx_copied[key], it * 2 + h + 1)
                        pool.nop(nofuse=True)
                        for u in range(by_pool(key)):
                            pool.indirect_dma_start(
                                ring[h][:, u, 0:width], None, table,
                                bass.IndirectOffsetOnAxis(ap=idx_ring[h][:, u:u + 1], axis=0),
                            ).then_inc(gathered[key][h], 16)

            pool.wait_ge(prep_taken, 6)
            gather("rel", relation_rows.rearrange("n (r f) -> (n r) f", r=R), rows, D, 5)
            def scatter(first, end):
                def step(it, first):
                    for h in range(2):
                        if not first:
                            pool.wait_ge(scattered[h], it * (16 * H))
                        cols = bass.ds(it * (2 * H) + h * H, H)
                        pool.tensor_copy(place_ring[h][:, :], idx_place[:, cols]).then_inc(records_copied, 1)
                        pool.tensor_copy(record_ring[h][:, :, :], records[:, cols, :]).then_inc(records_copied, 1)
                        pool.wait_ge(records_copied, it * 4 + 2 * h + 2)
                        pool.nop(nofuse=True)
                        for u in range(H):
                            pool.indirect_dma_start(
                                sorted_edges, bass.IndirectOffsetOnAxis(ap=place_ring[h][:, u:u + 1], axis=0),
                                record_ring[h][:, u, :], None).then_inc(scattered[h], 16)

                if first == 0:
                    step(0, True)
                    first = 1
                with pool.Fori(first, end) as it:
                    step(it, False)

            if layers > 1:
                gather("att", attention_rows, rows2, 2 * D, 1)
            if layers > 3:
                pool.wait_ge(records_ready, 1)
                scatter(0, SCATTER_STEPS[0])
            if layers > 2:
                gather("ch0", cheb_rows[0], rows, D, 1)
                if layers > 3:
                    scatter(*SCATTER_STEPS)
                gather("ch1", cheb_rows[1], rows, D, 1)
            if layers > 3:
                scatter(SCATTER_STEPS[1], IT)
                gather("gcn", support_rows, rows, D, 1)

        @block.scalar
        def _(act):
            def std(k):
                act.wait_ge(var_ready, k + 1)
                act.activation(stat[3][:, :, :], stat[2][:, :, :], ACT.Sqrt).then_inc(std_ready, 1)

            def take_turned(s, buf):
                for g in range(NG):
                    n = s * NG + g
                    w = min(GT, NB - g * GT) * P
                    act.wait_ge(turned, n + 1)
                    act.activation(hT[buf][:, g * GT * P:g * GT * P + w], work[n % 2][0:D, 0:w], ACT.Copy
                                   ).then_inc(turn_taken, 1)

            def copy_indices(index, it, h, sem):
                act.activation(idx_ring[h][:, :], index[:, bass.ds(it * (2 * H) + h * H, H)], ACT.Copy).then_inc(sem, 1)

            def split_messages(key, index=None):
                if index is not None:
                    for h in range(2):
                        copy_indices(index, 0, h, idx_copied[key])

                def step(it, last):
                    for h in range(2):
                        if key == "rel":
                            act.wait_ge(slot_free[key], it * 2 + h + 1)
                            source = rows[h]
                        else:
                            act.wait_ge(msg_ready[key], it * 2 + h + 1)
                            source = msg[h]
                        if index is not None:
                            act.wait_ge(gathered[key][h], (it + 1) * (16 * by_pool(key)))
                            if not last:
                                copy_indices(index, it + 1, h, idx_copied[key])
                        act.activation(parts[h][:, :, 0:D], source[:, :, :], ACT.Copy).then_inc(part1_ready[key], 1)
                        act.wait_ge(rest_ready[key], it * 2 + h + 1)
                        act.activation(parts[h][:, :, D:2 * D], rest[h][:, :, :], ACT.Copy).then_inc(part2_ready[key], 1)

                with act.Fori(0, IT - 1) as it:
                    step(it, False)
                step(IT - 1, True)

            std(0)
            take_turned(0, 0)
            split_messages("rel", idx_rel)
            act.wait_ge(var_ready, 2)
            act.activation(stat[3][:, :, :], stat[2][:, :, :], ACT.Sqrt).then_inc(std_ready, 1)
            if layers > 1:
                std(2)
                take_turned(1, 0)
                act.wait_ge(pd_ready, 1)
                for h in range(2):
                    copy_indices(idx_src, 0, h, idx_copied["att"])

                def attention_step(it, last):
                    for h in range(2):
                        act.wait_ge(gathered["att"][h], (it + 1) * (16 * H))
                        if not last:
                            copy_indices(idx_src, it + 1, h, idx_copied["att"])
                        act.activation(edge_rows[:, bass.ds(it * (2 * H) + h * H, H), 0:D], rows2[h][:, :, D:2 * D],
                                       ACT.Copy).then_inc(rows_kept, 1)
                        act.wait_ge(bank_read, it * 2 + h + 3)
                        act.activation(msg[h][:, :, :], msg[h][:, :, :], ACT.Tanh).then_inc(tanh_ready, 1)

                with act.Fori(0, IT - 1) as it:
                    attention_step(it, False)
                attention_step(IT - 1, True)
                act.wait_ge(expo_ready, 1)
                act.activation(weight_e[:, :], expo[:, :], ACT.Exp).then_inc(weight_ready, 1)
                split_messages("agg")
            if layers > 2:
                std(3)
                take_turned(2, 0)
                split_messages("ch0", idx_src)
                take_turned(3, 1)
                split_messages("ch1", idx_src)
                take_turned(4, 2)
                act.wait_ge(gates_ready, 1)
                act.activation(Tx1[:, :, :], stage[:, :, 0:D], ACT.Sigmoid, scale=-1.0).then_inc(gates_done, 1)
                act.activation(Tx2[:, :, :], stage[:, :, D:2 * D], ACT.Tanh).then_inc(gates_done, 1)
            if layers > 3:
                std(4)
                take_turned(5, 0)
                for c, to in enumerate((idx_dst, col_local_src, col_weight_sorted)):
                    act.wait_ge(sorted_turned, c + 1)
                    act.activation(to, work[(0, 1, 2)[c]][:, 0:T], ACT.Copy).then_inc(sorted_taken, 1)
                act.wait_ge(sorted_taken, 1)
                split_messages("gcn", idx_dst)

        @block.tensor
        def _(pe):
            def turn(s, src):
                pe.wait_ge(h_ready, s + 1)
                for g in range(NG):
                    n = s * NG + g
                    if n >= 2:
                        pe.wait_ge(turn_taken, n - 1)
                    for b in range(g * GT, min((g + 1) * GT, NB)):
                        c = (b - g * GT) * P
                        t = pe.transpose(work[n % 2][0:D, c:c + P], src[:, b, :], ident[:, :])
                    t.then_inc(turned, 1)

            def clear_sums(key, wait=None):
                if wait is not None:
                    pe.wait_ge(wait, 1)
                for i in range(ACC_BANKS):
                    m = pe.matmul(acc[:, i * BANK:(i + 1) * BANK], zeros[:, 0:P], zeros[:, :],
                                  start=True, stop=False, skip_group_check=True)
                    if i >= ACC_BANKS - 2:
                        m.then_inc(slot_free[key], 1)

            def add_up(key, counted=None):
                blocks = block_at if key != "gcn" else sorted_block_at

                def find(it):
                    pe.wait_ge(src_onehot_ready[key], it + 1)
                    for h in range(2):
                        pe.wait_ge(found_read[key], it * 2 + h + 1)
                        for b in range(NB):
                            m = pe.matmul(work[2 + h][:, 0:3 * D], onehot_src[:, b, h * P:(h + 1) * P],
                                          table_parts[:, b, :], start=(b == 0), stop=(b == NB - 1))
                        m.then_inc(found_ready[key], 1)

                def step(it, find_next):
                    for h in range(2):
                        _, at = nc.values_load_multi_w_load_instructions(
                            blocks[0:1, bass.ds(it * (2 * H) + h * H, H)], engines=[PE_ENGINE], min_val=0, max_val=NB - 1,
                            skip_runtime_bounds_check_because="a node's block, below NB")
                        pe.wait_ge(onehot_ready[key], it * 2 + h + 1)
                        for u in range(H):
                            there = acc[:, bass.ds(at[u] * D, 2 * D)]
                            if counted is not None:
                                n, what = counted(it, h * H + u)
                                counts_there = acc[:, bass.ds(at[u] * 3 + COUNTS, 6)]
                            for w in range(2):
                                hot = onehot[h][:, u, w * P:(w + 1) * P]
                                for k in range(3):
                                    m = pe.matmul(there[:, w * D:(w + 1) * D], hot,
                                                  parts[h][:, u, k * D:(k + 1) * D],
                                                  start=False, stop=False, skip_group_check=True)
                                if counted is not None:
                                    m = pe.matmul(counts_there[:, 3 * w:3 * w + n], hot, what,
                                                  start=False, stop=False, skip_group_check=True)
                            if key == "rel":
                                m = pe.matmul(work[0][:, 0:3 * NB], onehot_lo[h][:, u, :], hi_parts[h][:, u, :],
                                              start=False, stop=False, skip_group_check=True)
                        m.then_inc(slot_free[key], 1)
                        if h == 0 and find_next:
                            find(it + 1)

                if key not in HYBRID:
                    with pe.Fori(0, IT) as it:
                        step(it, False)
                else:
                    find(0)
                    with pe.Fori(0, IT - 1) as it:
                        step(it, True)
                    step(IT - 1, False)

            def look_up(key):
                for h in range(2):
                    pe.matmul(work[2 + h][:, :], zeros[:, 0:P], zeros[:, :], start=True, stop=True
                              ).then_inc(slot_free[key], 1)
                with pe.Fori(0, IT) as it:
                    for h in range(2):
                        _, at = nc.values_load_multi_w_load_instructions(
                            block_at[0:1, bass.ds(it * (2 * H) + h * H, H)], engines=[PE_ENGINE],
                            min_val=0, max_val=NB - 1,
                            skip_runtime_bounds_check_because="a node's block, below NB")
                        pe.wait_ge(onehot_ready[key], it * 2 + h + 1)
                        pe.wait_ge(bank_read, it * 2 + h + 1)
                        for u in range(H):
                            there = (attend_dst[:, :, :].rearrange("p b c -> p (b c)")
                                     [:, bass.ds(at[u] * (3 * D), 6 * D)])
                            for w in range(2):
                                for part in range(3):
                                    m = pe.matmul(work[2 + h][:, u * D:(u + 1) * D],
                                                  onehot_t[h][:, w, u * P:(u + 1) * P],
                                                  there[:, (3 * w + part) * D:(3 * w + part + 1) * D],
                                                  start=(w == 0 and part == 0), stop=False, skip_group_check=True)
                        m.then_inc(slot_free[key], 1)

            pe.wait_ge(consts_ready, CONSTS)
            turned_rows = [row_src, row_rel, row_local, row_hi, row_lo, raw_weight]
            for i, r in enumerate(turned_rows):
                pe.wait_ge(rows_derived, 2)
                if i >= 2:
                    pe.wait_ge(prep_taken, i - 1)
                for c in range(TC):
                    k = P if c < TC - 1 else TL
                    t = pe.transpose(work[i % 2][:, c * P:c * P + k], r[0:k, c, :], ident[0:k, 0:k])
                t.then_inc(prep_turned, 1)
            pe.wait_ge(prep_taken, 6)
            for i, r in enumerate((block_f[:, :, 0:1], ends[:, :, 0:1], ends[:, :, 1:2])):
                for c in range(TC):
                    k = P if c < TC - 1 else TL
                    t = pe.matmul(work[i][0:1, c * P:c * P + k], r[0:k, c, :], ident[0:k, 0:k], start=True, stop=True)
                t.then_inc(tile_rows_turned, 1)
            pe.wait_ge(params_loaded, 16 * 16)
            for i in range(2):
                t = pe.transpose(work[3][0:D, i * D:(i + 1) * D], w_attn[:, i * D:(i + 1) * D], ident[0:D, 0:D])
            t.then_inc(attn_w_turned, 1)

            pe.wait_ge(tile_info_ready, 1)
            pe.wait_ge(attn_w_taken, 1)
            turn(0, Hn)
            for b in range(NB):
                pe.wait_ge(turn_taken, b // GT + 1)
                if b >= 2:
                    pe.wait_ge(mm_taken[0], b - 1)
                pe.matmul(work[2 + b % 2][:, 0:R * D], hT[0][:, b * P:(b + 1) * P],
                          w_rel[:, :, :].rearrange("d r f -> d (r f)"), start=True, stop=True).then_inc(mm_done[0], 1)
            pe.matmul(work[0][:, 0:3 * NB], zeros[:, 0:P], zeros[:, 0:3 * NB], start=True, stop=False, skip_group_check=True)
            clear_sums("rel")
            add_up("rel", counted=lambda it, u: (1, ones_bf[:, :]))
            if layers > 1:
                pe.wait_ge(tile_counts_ready, 1)
                w = NB + 1
                for c in range(TC):
                    k = P if c < TC - 1 else TL
                    pe.matmul(work[2][:, c * w:(c + 1) * w], before[0:k, :], tile_counts[0:k, c, :],
                              start=True, stop=(c == 0), skip_group_check=True)
                    for d in range(c):
                        pe.matmul(work[2][:, c * w:(c + 1) * w], ones[:, :], tile_counts[:, d, :],
                                  start=False, stop=(d == c - 1), skip_group_check=True)
                for c in range(TC):
                    k = P if c < TC - 1 else TL
                    m = pe.matmul(work[3][:, 0:w], ones[0:k, :], tile_counts[0:k, c, :],
                                  start=(c == 0), stop=(c == TC - 1))
                m.then_inc(bases_ready, 1)
                turn(1, Hn)
                pe.wait_ge(bases_taken, 1)
                for g in range(NG):
                    pe.wait_ge(turn_taken, NG + g + 1)
                    if g >= 2:
                        pe.wait_ge(mm_taken[1], g - 1)
                    for b in range(g * GT, min((g + 1) * GT, NB)):
                        c = (b - g * GT) * P
                        m = pe.matmul(work[2 + g % 2][:, c:c + 2 * D], hT[0][:, b * P:(b + 1) * P],
                                      w_attn_t[:, :, :].rearrange("d a j -> d (a j)"), start=True, stop=True)
                    m.then_inc(mm_done[1], 1)
                pe.wait_ge(pd_ready, 1)
                pe.wait_ge(mm_taken[1], NG)
                look_up("att")
                pe.wait_ge(places_ready, 1)
                for c in range(TC):
                    k = P if c < TC - 1 else TL
                    t = pe.transpose(work[0][:, c * P:c * P + k], place[0:k, c, :], ident[0:k, 0:k])
                for c in range(TC):
                    k = P if c < TC - 1 else TL
                    t = pe.matmul(work[1][0:1, c * P:c * P + k], sorted_block[0:k, c, :], ident[0:k, 0:k],
                                  start=True, stop=True)
                t = pe.matmul(work[3][:, 0:T], ones[0:1, :], tile_base[0:1, :], start=True, stop=True)
                t.then_inc(places_turned, 1)
                pe.wait_ge(records_ready, 1)
                pe.wait_ge(shifted_ready, 1)
                for c in range(TC):
                    k = P if c < TC - 1 else TL
                    t = pe.transpose(work[0][0:k, c * P:(c + 1) * P], shifted[:, c * P:c * P + k], ident[:, :])
                t.then_inc(scores_turned, 1)
                pe.wait_ge(edge_vals_ready, 1)
                for i, r in enumerate((prefix[:, :, P - 1:P], suffix[:, :, 0:1])):
                    for c in range(TC):
                        k = P if c < TC - 1 else TL
                        t = pe.matmul(work[2 + i][0:1, c * P:c * P + k], r[0:k, c, :], ident[0:k, 0:k],
                                      start=True, stop=True)
                t.then_inc(edge_vals_turned, 1)
                pe.wait_ge(carries_ready, 1)
                for i in range(2):
                    for c in range(TC):
                        k = P if c < TC - 1 else TL
                        t = pe.matmul(work[1][0:k, i * TC + c:i * TC + c + 1], carries[0:1, i, c * P:c * P + k],
                                      ident[0:1, 0:1], start=True, stop=True)
                t.then_inc(carries_turned, 1)
                pe.wait_ge(max_ready, 1)
                for c in range(TC):
                    k = P if c < TC - 1 else TL
                    t = pe.transpose(work[2][:, c * P:c * P + k], prefix[0:k, c, :], ident[0:k, 0:k])
                t.then_inc(max_turned, 1)
                clear_sums("agg", sums_taken["rel"])
                add_up("agg", counted=lambda it, u: (3, count_parts[:, bass.ds(it * (2 * H) + u, 1), :]
                                                     .rearrange("p a c -> p (a c)")))

            if layers > 2:
                for i, (key, mat) in enumerate((("ch0", Hn), ("ch1", Tx1))):
                    turn(2 + i, mat)
                    clear_sums(key, sums_taken["agg"] if i == 0 else None)
                    add_up(key)
                turn(4, Tx2)
                for g in range(NG):
                    pe.wait_ge(turn_taken, 4 * NG + g + 1)
                    if g >= 2:
                        pe.wait_ge(mm_taken[2], g - 1)
                    for b in range(g * GT, min((g + 1) * GT, NB)):
                        c = (b - g * GT) * P
                        for k in range(3):
                            m = pe.matmul(work[2 + g % 2][:, c:c + 2 * D], hT[k][:, b * P:(b + 1) * P],
                                          w_cheb[:, k, :, :].rearrange("d g f -> d (g f)"), start=(k == 0), stop=(k == 2))
                    m.then_inc(mm_done[2], 1)

            if layers > 3:
                turn(5, Hn)
                for g in range(NG):
                    pe.wait_ge(turn_taken, 5 * NG + g + 1)
                    if g >= 2:
                        pe.wait_ge(mm_taken[3], g - 1)
                    for b in range(g * GT, min((g + 1) * GT, NB)):
                        c = (b - g * GT) * D
                        m = pe.matmul(work[2 + g % 2][:, c:c + D], hT[0][:, b * P:(b + 1) * P], w_gcn[:, :],
                                      start=True, stop=True)
                    m.then_inc(mm_done[3], 1)
                pe.wait_ge(mm_taken[3], NG)
                pe.wait_ge(sorted_rows_ready, 1)
                for i, r in enumerate((row_dst_sorted, row_local_src, row_weight_sorted)):
                    for c in range(TC):
                        k = P if c < TC - 1 else TL
                        t = pe.transpose(work[i][:, c * P:c * P + k], r[0:k, c, :], ident[0:k, 0:k])
                    t.then_inc(sorted_turned, 1)
                clear_sums("gcn", sums_taken["ch1"])
                add_up("gcn")

        @block.vector
        def _(dve):
            steps = [0]

            def then(ins):
                steps[0] += 1
                ins.then_inc(vec, 1)
                dve.wait_ge(vec, steps[0])

            def per_node(a):
                return a[:, :, :].to_broadcast([P, NB, D])

            def layernorm(k, sqrt_no):
                then(dve.tensor_reduce(stat[0][:, :, :], X[:, :, :], AX.X, ALU.add))
                then(dve.tensor_single_scalar(stat[1][:, :, :], stat[0][:, :, :], 1.0 / D, ALU.mult))
                then(dve.tensor_tensor(xc[:, :, :], X[:, :, :], per_node(stat[1]), ALU.subtract))
                then(dve.tensor_tensor(sq[:, :, :], xc[:, :, :], xc[:, :, :], ALU.mult))
                then(dve.tensor_reduce(stat[0][:, :, :], sq[:, :, :], AX.X, ALU.add))
                dve.tensor_scalar(stat[2][:, :, :], stat[0][:, :, :], 1.0 / D, EPS, ALU.mult, ALU.add).then_inc(var_ready, 1)
                dve.wait_ge(std_ready, sqrt_no)
                then(dve.reciprocal(stat[4][:, :, :], stat[3][:, :, :]))
                then(dve.tensor_tensor(sq[:, :, :], xc[:, :, :], per_node(stat[4]), ALU.mult))
                dve.tensor_single_scalar(Hn[:, :, :], sq[:, :, :], 0.0, ALU.max).then_inc(h_ready, 1)

            def split():
                part = [attend_dst[:, 0:NB, k * D:(k + 1) * D] for k in range(3)]
                then(dve.tensor_copy(part[0], pd))
                then(dve.tensor_tensor(pd_rest, pd, part[0], ALU.subtract))
                then(dve.tensor_copy(part[1], pd_rest))
                dve.tensor_tensor(part[2], pd_rest, part[1], ALU.subtract).then_inc(pd_ready, 1)

            def onehot_rows(key, here, it, h):
                dve.wait_ge(here[h], (it + 1) * 16)
                dve.wait_ge(slot_free[key], it * 2 + h + 1)
                for w in range(2):
                    o = dve.tensor_scalar(onehot_t[h][:, w, :], local_ring[h][:, :], iota_part[:, w:w + 1], None,
                                          ALU.is_equal)
                o.then_inc(onehot_ready[key], 1)

            def count_block(it):
                K = 5
                dve.tensor_scalar(in_block, row_hi[:, :, :], iota_row[:, bass.ds(it, 1)], None, ALU.is_equal
                                  ).then_inc(rank_step, 1)
                dve.wait_ge(rank_step, it * K + 1)
                dve.tensor_tensor_scan(running.rearrange("p c e -> p (c e)"), keep_run.rearrange("p c e -> p (c e)"),
                                       in_block.rearrange("p c e -> p (c e)"), 0.0, ALU.mult, ALU.add
                                       ).then_inc(rank_step, 1)
                dve.wait_ge(rank_step, it * K + 2)
                dve.tensor_tensor(picked, in_block, running, ALU.mult).then_inc(rank_step, 1)
                dve.tensor_copy(tile_counts[:, :, bass.ds(it, 1)], running[:, :, P - 1:P]).then_inc(rank_step, 1)
                dve.wait_ge(rank_step, it * K + 4)
                dve.tensor_tensor(place[:, :, :], place[:, :, :], picked, ALU.add).then_inc(rank_step, 1)
                dve.wait_ge(rank_step, it * K + K)

            def place_block(it):
                dve.scalar_tensor_tensor(picked, row_hi[:, :, :], iota_row[:, bass.ds(it, 1)],
                                         place_base[:, :, bass.ds(it, 1)].to_broadcast([P, TC, P]),
                                         ALU.is_equal, ALU.mult).then_inc(place_step, 1)
                dve.wait_ge(place_step, it * 2 + 1)
                dve.tensor_tensor(place[:, :, :], place[:, :, :], picked, ALU.add).then_inc(place_step, 1)
                dve.wait_ge(place_step, it * 2 + 2)

            def split_rest(key, it, h, source):
                dve.wait_ge(part1_ready[key], it * 2 + h + 1)
                return dve.tensor_tensor(rest[h][:, :, :], source[:, :, :], parts[h][:, :, 0:D], ALU.subtract
                                         ).then_inc(rest_ready[key], 1)

            def split_last(key, it, h):
                dve.wait_ge(part2_ready[key], it * 2 + h + 1)
                return dve.tensor_tensor(parts[h][:, :, 2 * D:3 * D], rest[h][:, :, :], parts[h][:, :, D:2 * D],
                                         ALU.subtract)

            def split_table():
                part = [table_parts[:, :, k * D:(k + 1) * D] for k in range(3)]
                then(dve.tensor_copy(part[0], stage[:, :, 0:D]))
                then(dve.tensor_tensor(pd_rest, stage[:, :, 0:D], part[0], ALU.subtract))
                then(dve.tensor_copy(part[1], pd_rest))
                then(dve.tensor_tensor(part[2], pd_rest, part[1], ALU.subtract))

            def source_onehots(key, it):
                dve.wait_ge(wanted_here[key], (it + 1) * 16)
                for b in range(NB):
                    o = dve.tensor_scalar(onehot_src[:, b, :], wanted.rearrange("p a e -> p (a e)"), iota_part[:, b:b + 1],
                                          None, ALU.is_equal)
                o.then_inc(src_onehot_ready[key], 1)

            def make_messages(key, weight, local=col_local):
                if key != "agg":
                    dve.sem_inc(rows_free[key], 2)

                def step(it, find_next):
                    for h in range(2):
                        cols = bass.ds(it * (2 * H) + h * H, H)
                        dve.wait_ge(slot_free[key], it * 2 + h + 1)
                        if key != "agg":
                            dve.wait_ge(gathered[key][h], (it + 1) * (16 * by_pool(key)))
                        if key in HYBRID:
                            dve.wait_ge(found_ready[key], it * 2 + h + 1)
                            dve.tensor_reduce(rows[h][:, H - 1, :],
                                              work[2 + h][:, 0:3 * D].rearrange("p (k d) -> p d k", k=3),
                                              AX.X, ALU.add).then_inc(found_read[key], 1)
                            dve.wait_ge(found_read[key], it * 2 + h + 3)
                        if key == "rel":
                            source = rows[h]
                        else:
                            source = msg[h]
                            given = rows[h][:, :, :] if key != "agg" else edge_rows[:, cols, :]
                            o = dve.tensor_tensor(msg[h][:, :, :], given,
                                                  weight[:, cols].unsqueeze(2).to_broadcast([P, H, D]), ALU.mult
                                                  )
                            o.then_inc(msg_ready[key], 1)
                            if key != "agg":
                                dve.wait_ge(msg_ready[key], it * 2 + h + 1)
                                dve.sem_inc(rows_free[key], 1)
                        if key == "rel":
                            dve.tensor_tensor(onehot_hi[h][:, :, :],
                                              iota_row[:, 0:NB].unsqueeze(1).to_broadcast([P, H, NB]),
                                              col_hi[:, cols].unsqueeze(2).to_broadcast([P, H, NB]),
                                              ALU.is_equal).then_inc(hi_ready, 1)
                        for u in range(H):
                            col = bass.ds(it * (2 * H) + (h * H + u), 1)
                            dve.tensor_scalar(onehot[h][:, u, :], iota_bf[:, :], local[:, col], None, ALU.is_equal)
                            if key == "rel":
                                dve.tensor_scalar(onehot_lo[h][:, u, :], iota_bf[:, 0:P], col_lo[:, col], None, ALU.is_equal)
                            if u == H // 2 - 1:
                                split_rest(key, it, h, source)
                                if key == "rel":
                                    dve.wait_ge(rest_ready[key], it * 2 + h + 1)
                                    dve.sem_inc(rows_free[key], 1)
                        if key == "rel":
                            dve.wait_ge(hi_ready, it * 2 + h + 1)
                            dve.tensor_tensor(hi_parts[h].rearrange("p t (k b) -> p t k b", k=3),
                                              onehot_hi[h].unsqueeze(2).to_broadcast([P, H, 3, NB]),
                                              degree_parts[:, cols, :].unsqueeze(3).to_broadcast([P, H, 3, NB]), ALU.mult)
                        split_last(key, it, h).then_inc(onehot_ready[key], 1)
                        if h == 0 and find_next:
                            dve.wait_ge(found_ready[key], it * 2 + 2)
                            source_onehots(key, it + 1)
                    if key == "rel":
                        count_block(it)

                if key not in HYBRID:
                    with dve.Fori(0, IT) as it:
                        step(it, False)
                else:
                    dve.wait_ge(table_staged, HYBRID.index(key) + 2)
                    split_table()
                    dve.sem_inc(found_read[key], 2)
                    source_onehots(key, 0)
                    with dve.Fori(0, IT - 1) as it:
                        step(it, True)
                    step(IT - 1, False)

            S = acc[:, 0:NB * D].rearrange("p (b d) -> p b d", b=NB)
            count = stat[5]

            def take_counts():
                then(dve.tensor_reduce(count[:, :, :], acc[:, COUNTS:COUNTS + 3 * NB].rearrange("p (b k) -> p b k", k=3),
                                       AX.X, ALU.add))

            def split_columns(values, three, rest):
                v = values[:, :].unsqueeze(2)
                then(dve.tensor_copy(three[:, :, 0:1], v))
                then(dve.tensor_tensor(rest, v, three[:, :, 0:1], ALU.subtract))
                then(dve.tensor_copy(three[:, :, 1:2], rest))
                then(dve.tensor_tensor(three[:, :, 2:3], rest, three[:, :, 1:2], ALU.subtract))

            dve.wait_ge(raw_loaded, RAW_LOADS * 16)
            then(dve.tensor_single_scalar(block_i[:, :, :], raw_dst[:, :, 0:1], P.bit_length() - 1, ALU.logical_shift_right))
            then(dve.tensor_copy(block_f[:, :, :], block_i[:, :, :]))
            then(dve.tensor_single_scalar(block_first[:, :, :], block_f[:, :, :], float(P), ALU.mult))
            then(dve.tensor_tensor(row_local[:, :, :], raw_dst[:, :, :], block_first[:, :, :].to_broadcast([P, TC, P]),
                                   ALU.subtract))
            dve.tensor_copy(local_bf[:, :, :], row_local[:, :, :]).then_inc(rows_derived, 1)
            dve.tensor_single_scalar(src_hi_i[:, :, :], raw_src[:, :, :], P.bit_length() - 1, ALU.logical_shift_right)
            then(dve.tensor_single_scalar(src_lo_i[:, :, :], raw_src[:, :, :], P - 1, ALU.bitwise_and))
            dve.tensor_copy(row_hi[:, :, :], src_hi_i[:, :, :])
            dve.tensor_copy(row_lo[:, :, :], src_lo_i[:, :, :])
            dve.tensor_copy(row_src[:, :, :], raw_src[:, :, :])
            dve.tensor_copy(src_i16, raw_src[:, :, :])
            dve.tensor_copy(ends[:, :, 0:1], raw_dst[:, :, 0:1])
            dve.tensor_copy(ends[:, :, 1:2], raw_dst[:, :, P - 1:P])
            same3 = same.rearrange("p (c e) -> p c e", c=TC)
            dve.memset(same3[:, :, 0:1], 0.0)
            dve.tensor_tensor(same3[:, :, 1:P], raw_dst[:, :, 1:P], raw_dst[:, :, 0:P - 1], ALU.is_equal)
            dve.scalar_tensor_tensor(row_rel[:, :, :], raw_src[:, :, :], float(R), raw_type[:, :, :], ALU.mult, ALU.add
                                     ).then_inc(rows_derived, 1)
            for i, c in enumerate((idx_src, idx_rel, col_local, col_hi, col_lo, col_weight)):
                dve.wait_ge(prep_turned, i + 1)
                dve.tensor_copy(c[:, :], work[i % 2][:, 0:T]).then_inc(prep_taken, 1)
            dve.wait_ge(prep_taken, 6)
            split_columns(col_weight, degree_parts, degree_rest)
            dve.wait_ge(tile_rows_turned, 3)
            then(dve.tensor_copy(tile_block[0:1, :], work[0][0:1, 0:T]))
            dve.tensor_copy(tile_ends[0:1, 0, :], work[1][0:1, 0:T])
            dve.tensor_copy(tile_ends[0:1, 1, :], work[2][0:1, 0:T])
            then(dve.tensor_copy(block_at[:, :], tile_block[0:1, :]))
            dve.tensor_tensor(whole[:, :], tile_ends[0:1, 0, :], tile_ends[0:1, 1, :], ALU.is_equal)
            dve.tensor_tensor(link[:, 1:T], tile_ends[0:1, 0, 1:T], tile_ends[0:1, 1, 0:T - 1], ALU.is_equal)
            dve.memset(link[:, 0:1], 0.0).then_inc(tile_info_ready, 1)
            dve.wait_ge(attn_w_turned, 1)
            dve.tensor_copy(w_attn_t[:, :, :].rearrange("d a j -> d (a j)"), work[3][0:D, 0:2 * D]).then_inc(attn_w_taken, 1)

            dve.wait_ge(x_loaded, 32)
            layernorm(0, 1)
            for b in range(NB):
                dve.wait_ge(mm_done[0], b + 1)
                dve.tensor_copy(relation_stage[:, b, :], work[2 + b % 2][:, 0:R * D]).then_inc(mm_taken[0], 1)
            dve.memset(keep_run[:, :, 1:P], 1.0)
            dve.memset(keep_run[:, :, 0:1], 0.0)
            then(dve.memset(place[:, :, :], 0.0))
            make_messages("rel", None)
            dve.wait_ge(rank_step, IT * 5)
            then(dve.memset(block_total[:, :], 1.0))
            dve.sem_inc(tile_counts_ready, 1)
            dve.wait_ge(slot_free["rel"], FREED)
            take_counts()
            then(dve.tensor_single_scalar(stat[0][:, :, :], count[:, :, :], 1.0, ALU.max))
            then(dve.tensor_single_scalar(stat[1][:, :, :], count[:, :, :], 1.0, ALU.min))
            then(dve.reciprocal(stat[4][:, :, :], stat[0][:, :, :]))
            dve.tensor_tensor(xc[:, :, :], S, per_node(stat[4]), ALU.mult).then_inc(sums_taken["rel"], 1)
            dve.wait_ge(sums_taken["rel"], 1)
            then(dve.tensor_single_scalar(sq[:, :, :], xc[:, :, :], 1.0 - KEEP, ALU.mult))
            then(dve.scalar_tensor_tensor(xc[:, :, :], Hn[:, :, :], KEEP, sq[:, :, :], ALU.mult, ALU.add))
            then(dve.scalar_tensor_tensor(sq[:, :, :], xc[:, :, :], 0.0, Hn[:, :, :], ALU.max, ALU.subtract))
            then(dve.tensor_tensor(xc[:, :, :], sq[:, :, :], per_node(stat[1]), ALU.mult))
            then(dve.tensor_tensor(sq[:, :, :], xc[:, :, :], Hn[:, :, :], ALU.add))
            then(dve.tensor_tensor(X[:, :, :], X[:, :, :], sq[:, :, :], ALU.add))
            then(dve.tensor_reduce(stat[5][:, :, :], work[0][:, 0:3 * NB].rearrange("p (k b) -> p b k", k=3), AX.X, ALU.add))
            then(dve.tensor_single_scalar(stat[1][:, :, :], stat[5][:, :, :], 0.0, ALU.is_gt))
            then(dve.tensor_tensor(stat[0][:, :, :], stat[5][:, :, :], stat[1][:, :, :], ALU.mult))
            then(dve.tensor_scalar(stat[4][:, :, :], stat[1][:, :, :], -1.0, 1.0, ALU.mult, ALU.add))
            dve.tensor_tensor(stat[2][:, :, :], stat[0][:, :, :], stat[4][:, :, :], ALU.add).then_inc(var_ready, 1)
            dve.wait_ge(std_ready, 2)
            then(dve.reciprocal(stat[0][:, :, :], stat[3][:, :, :]))
            then(dve.tensor_tensor(dis[:, :, :], stat[0][:, :, :], stat[1][:, :, :], ALU.mult))
            then(dve.tensor_single_scalar(neg_dis[:, :, :], dis[:, :, :], -1.0, ALU.mult))

            if layers > 1:
                dve.wait_ge(bases_ready, 1)
                then(dve.tensor_copy(block_start[:, :], work[3][:, 0:NB + 1]))
                then(dve.tensor_tensor_scan(block_total[:, :], ones[:, 0:NB + 1], block_start[:, :], 0.0, ALU.mult, ALU.add))
                then(dve.tensor_tensor(block_start[:, :], block_total[:, :], block_start[:, :], ALU.subtract))
                dve.tensor_tensor(place_base[:, :, :], work[2][:, 0:TC * (NB + 1)].rearrange("p (c b) -> p c b", c=TC),
                                  block_start[:, :].unsqueeze(1).to_broadcast([P, TC, NB + 1]), ALU.add
                                  ).then_inc(bases_taken, 1)
                dve.wait_ge(bases_taken, 1)
                layernorm(1, 3)
                for g in range(NG):
                    bs = slice(g * GT, min((g + 1) * GT, NB))
                    n = bs.stop - bs.start
                    dve.wait_ge(mm_done[1], g + 1)
                    got = work[2 + g % 2][:, 0:n * 2 * D].rearrange("p (b a j) -> p b a j", b=n, a=2)
                    dve.tensor_copy(stage[:, bs, 0:D], got[:, :, 0, :])
                    dve.tensor_tensor(pd[:, bs, :], got[:, :, 1, :], b_attn[:, :].unsqueeze(1).to_broadcast([P, n, D]),
                                      ALU.add).then_inc(mm_taken[1], 1)
                dve.wait_ge(h_ready, 2)
                dve.tensor_copy(stage[:, :, D:2 * D], Hn[:, :, :]).then_inc(table_staged, 1)
                dve.wait_ge(mm_taken[1], NG)
                split()
                then(dve.scalar_tensor_tensor(rest[0][:, 0, :], w_out[:, :], -1.0, w_out[:, :], ALU.mult, ALU.max))
                then(dve.tensor_reduce(above[:, :], rest[0][:, 0, :], AX.X, ALU.add))
                then(dve.tensor_scalar(above[:, :], above[:, :], 1.0 + 2.0 ** -10, 1.0, ALU.mult, ALU.add))
                dve.sem_inc(rows_free["att"], 2)
                dve.sem_inc(bank_read, 2)

                onehot_rows("att", local_here, 0, 0)

                def score_step(it, last):
                    for h in range(2):
                        if h == 0:
                            onehot_rows("att", local_here, it, 1)
                        elif not last:
                            onehot_rows("att", local_here, it + 1, 0)
                        dve.wait_ge(gathered["att"][h], (it + 1) * (16 * H))
                        dve.wait_ge(slot_free["att"], it * 2 + h + 3)
                        dve.tensor_tensor(msg[h][:, :, :], work[2 + h][:, :].rearrange("p (t d) -> p t d", t=H),
                                          rows2[h][:, :, 0:D], ALU.add).then_inc(bank_read, 1)
                        dve.wait_ge(bank_read, it * 2 + h + 3)
                        dve.wait_ge(rows_kept, it * 2 + h + 1)
                        dve.sem_inc(rows_free["att"], 1)
                        dve.wait_ge(tanh_ready, it * 2 + h + 1)
                        dve.tensor_tensor(rest[h][:, :, :], msg[h][:, :, :],
                                          w_out[:, :].unsqueeze(1).to_broadcast([P, H, D]), ALU.mult
                                          ).then_inc(prod_ready, 1)
                        dve.wait_ge(prod_ready, it * 2 + h + 1)
                        dve.tensor_reduce(score[:, bass.ds(it * (2 * H) + h * H, H)], rest[h][:, :, :], AX.X, ALU.add
                                          ).then_inc(scores_ready, 1)
                    place_block(it)

                with dve.Fori(0, IT - 1) as it:
                    score_step(it, False)
                score_step(IT - 1, True)
                dve.wait_ge(place_step, IT * 2)
                dve.tensor_single_scalar(place[:, :, :], place[:, :, :], 1.0, ALU.subtract)
                for c in range(TC):
                    dve.tensor_scalar(sorted_first[:, c, :], iota_part[:, 0:1], float(P), float(c * P * P), ALU.mult, ALU.add)
                dve.wait_ge(slot_free["att"], FREED)
                then(dve.tensor_copy(tile_base[0:1, :], block_at[0:1, :]))
                then(dve.tensor_single_scalar(tile_base[0:1, :], tile_base[0:1, :], float(P), ALU.mult))
                then(dve.tensor_tensor(starts_here[:, :, :], block_start[:, :].unsqueeze(1).to_broadcast([P, TC, NB + 1]),
                                       sorted_first[:, :, :].to_broadcast([P, TC, NB + 1]), ALU.is_le))
                then(dve.tensor_reduce(sorted_block[:, :, :], starts_here[:, :, :], AX.X, ALU.add))
                dve.tensor_single_scalar(sorted_block[:, :, :], sorted_block[:, :, :], 1.0, ALU.subtract
                                         ).then_inc(places_ready, 1)
                dve.tensor_copy(records[:, :, 0:1], idx_src[:, :].unsqueeze(2))
                dve.tensor_copy(records[:, :, 2:3], col_weight[:, :].unsqueeze(2))
                dve.wait_ge(places_turned, 1)
                dve.tensor_copy(idx_place, work[0][:, 0:T])
                dve.tensor_copy(sorted_block_at[0:1, :], work[1][0:1, 0:T])
                then(dve.tensor_tensor(records[:, :, 1:2], col_local[:, :].unsqueeze(2), work[3][:, 0:T].unsqueeze(2), ALU.add))
                dve.tensor_single_scalar(records[:, :, 1:2], records[:, :, 1:2], float(NB * P - 1), ALU.min
                                         ).then_inc(records_ready, 1)
                dve.wait_ge(scores_ready, 2 * IT)
                dve.memset(V[:, TC - 1, :], 0.0)
                dve.tensor_scalar(shifted, score[:, :], above[:, 0:1], None, ALU.add).then_inc(shifted_ready, 1)
                dve.wait_ge(scores_turned, 1)
                dve.tensor_copy(V[:, 0:TC - 1, :], work[0][:, 0:(TC - 1) * P].rearrange("p (c e) -> p c e", c=TC - 1))
                then(dve.tensor_copy(V[0:TL, TC - 1, :], work[0][0:TL, (TC - 1) * P:TC * P]))

                def flat(a):
                    return a.rearrange("p c e -> p (c e)")

                def scans():
                    dve.tensor_tensor_scan(flat(prefix), same, flat(V), 0.0, ALU.mult, ALU.max)
                    return dve.tensor_tensor_scan(flat(suffix)[:, ::-1], same_next[:, ::-1], flat(V)[:, ::-1], 0.0,
                                                  ALU.mult, ALU.max)

                scans().then_inc(edge_vals_ready, 1)
                dve.memset(carry_f[0:1, :, :], 0.0)
                then(dve.memset(carry_b[0:1, :, :], 0.0))
                dve.tensor_tensor(carry_f[0:1, 0, 1:T], link[:, 1:T], whole[:, 0:T - 1], ALU.mult)
                dve.tensor_tensor(carry_b[0:1, 0, 0:T - 1], link[:, 1:T], whole[:, 1:T], ALU.mult)
                dve.wait_ge(edge_vals_turned, 1)
                dve.tensor_tensor(carry_f[0:1, 1, 1:T], link[:, 1:T], work[2][0:1, 0:T - 1], ALU.mult)
                then(dve.tensor_tensor(carry_b[0:1, 1, 0:T - 1], link[:, 1:T], work[3][0:1, 1:T], ALU.mult))
                dve.tensor_tensor_scan(carries[:, 0, :], carry_f[0:1, 0, :], carry_f[0:1, 1, :], 0.0, ALU.mult, ALU.max)
                dve.tensor_tensor_scan(carries[:, 1, :][:, ::-1], carry_b[0:1, 0, :][:, ::-1], carry_b[0:1, 1, :][:, ::-1],
                                       0.0, ALU.mult, ALU.max).then_inc(carries_ready, 1)
                dve.wait_ge(carries_turned, 1)
                dve.tensor_copy(carry_cols[:, :, 0:TC - 1], work[1][:, 0:2 * TC].rearrange("p (i c) -> p i c", i=2)[:, :, 0:TC - 1])
                then(dve.tensor_copy(carry_cols[0:TL, :, TC - 1:TC],
                                     work[1][0:TL, 0:2 * TC].rearrange("p (i c) -> p i c", i=2)[:, :, TC - 1:TC]))
                for i, e in enumerate((0, P - 1)):
                    for rows_, cs in ((P, slice(0, TC - 1)), (TL, slice(TC - 1, TC))):
                        then(dve.tensor_tensor(V[0:rows_, cs, e], V[0:rows_, cs, e], carry_cols[0:rows_, i, cs], ALU.max))
                then(scans())
                dve.tensor_tensor(flat(prefix), flat(prefix), flat(suffix), ALU.max).then_inc(max_ready, 1)
                dve.wait_ge(max_turned, 1)
                then(dve.tensor_scalar(shift, work[2][:, 0:T], above[:, 0:1], None, ALU.subtract))
                dve.tensor_tensor(expo, score[:, :], shift, ALU.subtract).then_inc(expo_ready, 1)
                dve.wait_ge(weight_ready, 1)
                split_columns(weight_e, count_parts, weight_rest)
                make_messages("agg", weight_e)
                dve.wait_ge(slot_free["agg"], FREED)
                take_counts()
                then(dve.tensor_single_scalar(stat[0][:, :, :], count[:, :, :], 0.0, ALU.is_equal))
                then(dve.tensor_tensor(stat[1][:, :, :], stat[0][:, :, :], count[:, :, :], ALU.add))
                then(dve.reciprocal(stat[4][:, :, :], stat[1][:, :, :]))
                dve.tensor_tensor(xc, S, per_node(stat[4]), ALU.mult).then_inc(sums_taken["agg"], 1)
                dve.wait_ge(sums_taken["agg"], 1)
                then(dve.tensor_tensor(X[:, :, :], X[:, :, :], xc, ALU.add))

            if layers > 2:
                layernorm(2, 4)
                dve.wait_ge(h_ready, 3)
                dve.tensor_tensor(stage[:, :, 0:D], Hn[:, :, :], per_node(dis), ALU.mult).then_inc(table_staged, 1)
                then(dve.tensor_tensor(bias_cheb[:, :, :], b_cheb[:, 0, :, :], b_cheb[:, 1, :, :], ALU.add))
                make_messages("ch0", col_weight)
                dve.wait_ge(slot_free["ch0"], FREED)
                dve.tensor_tensor(Tx1[:, :, :], S, per_node(neg_dis), ALU.mult).then_inc(h_ready, 1)
                dve.wait_ge(h_ready, 4)
                dve.tensor_tensor(stage[:, :, 0:D], Tx1[:, :, :], per_node(dis), ALU.mult).then_inc(table_staged, 1)
                make_messages("ch1", col_weight)
                dve.wait_ge(slot_free["ch1"], FREED)
                then(dve.tensor_single_scalar(stat[0][:, :, :], neg_dis[:, :, :], 2.0, ALU.mult))
                dve.tensor_tensor(sq, S, per_node(stat[0]), ALU.mult).then_inc(sums_taken["ch1"], 1)
                dve.wait_ge(sums_taken["ch1"], 1)
                dve.tensor_tensor(Tx2[:, :, :], sq, Hn[:, :, :], ALU.subtract).then_inc(h_ready, 1)
                for g in range(NG):
                    bs = slice(g * GT, min((g + 1) * GT, NB))
                    n = bs.stop - bs.start
                    dve.wait_ge(mm_done[2], g + 1)
                    o = dve.tensor_tensor(stage[:, bs, :], work[2 + g % 2][:, 0:n * 2 * D].rearrange("p (b c) -> p b c", b=n),
                                          bias_cheb[:, :, :].rearrange("p a d -> p (a d)").unsqueeze(1)
                                          .to_broadcast([P, n, 2 * D]), ALU.add)
                    o.then_inc(mm_taken[2], 1)
                dve.wait_ge(mm_taken[2], NG)
                dve.memset(stat[5][:, :, :], 0.0).then_inc(gates_ready, 1)
                dve.wait_ge(gates_done, 2)
                then(dve.tensor_tensor(xc, Tx1[:, :, :], Tx2[:, :, :], ALU.mult))
                then(dve.tensor_tensor(X[:, :, :], X[:, :, :], xc, ALU.add))

            if layers > 3:
                layernorm(3, 5)
                for g in range(NG):
                    bs = slice(g * GT, min((g + 1) * GT, NB))
                    n = bs.stop - bs.start
                    dve.wait_ge(mm_done[3], g + 1)
                    dve.tensor_copy(stage[:, bs, 0:D], work[2 + g % 2][:, 0:n * D].rearrange("p (b c) -> p b c", b=n)
                                    ).then_inc(mm_taken[3], 1)
                dve.wait_ge(mm_taken[3], NG)
                dve.tensor_tensor(X[:, :, :], X[:, :, :], b_gcn[:, :].unsqueeze(1).to_broadcast([P, NB, D]), ALU.add
                                  ).then_inc(table_staged, 1)
                dve.wait_ge(sorted_loaded, 32)
                then(dve.tensor_single_scalar(sorted_first[:, :, :], sorted_block[:, :, :], float(P), ALU.mult))
                for rows_, cs, n in ((P, slice(0, TC - 1), TC - 1), (TL, slice(TC - 1, TC), 1)):
                    got = sorted_rows[0:rows_, cs, :].rearrange("t c (e j) -> t c e j", j=3)
                    dve.tensor_tensor(row_local_src[0:rows_, cs, :], got[:, :, :, 0],
                                      sorted_first[0:rows_, cs, :].to_broadcast([rows_, n, P]), ALU.subtract)
                    dve.tensor_copy(row_dst_sorted[0:rows_, cs, :], got[:, :, :, 1])
                    dve.tensor_copy(dst_i16[0:rows_, cs, :], got[:, :, :, 1])
                    o = dve.tensor_copy(row_weight_sorted[0:rows_, cs, :], got[:, :, :, 2])
                o.then_inc(sorted_rows_ready, 1)
                dve.wait_ge(sorted_taken, 3)
                make_messages("gcn", col_weight_sorted, col_local_src)
                dve.wait_ge(slot_free["gcn"], FREED)
                then(dve.tensor_tensor(X[:, :, :], X[:, :, :], S, ALU.add))
            dve.memset(stat[5][:, :, :], 0.0).then_inc(out_ready, 1)

        return nc


_INS = ["x", "src", "dst", "edge_type_8", "edge_weight", "L0_gnn_weight_r", "L1_gnn_W_attn", "L1_gnn_b_attn",
        "L1_gnn_w_out", "L2_gnn_Wxz", "L2_gnn_bxz", "L2_gnn_bhz", "L2_gnn_Wxh", "L2_gnn_bxh", "L2_gnn_bhh",
        "L3_gnn_weight", "L3_gnn_bias"]


def kernel(**inputs):
    import numpy as np
    import concourse.bacc as bacc
    from concourse.bass_utils import run_bass_kernel_spmd

    nc = bacc.Bacc("TRN2", target_bir_lowering=False, num_devices=1)
    arrays = {f"in_{n}": np.ascontiguousarray(inputs[n]) for n in _INS}
    aps = {n: nc.dram_tensor(f"in_{n}", arrays[f"in_{n}"].shape, mybir.dt.from_np(arrays[f"in_{n}"].dtype),
                             kind="ExternalInput").ap() for n in _INS}
    shape = inputs["x"].shape
    out = nc.dram_tensor("out_x", shape, F32, kind="ExternalOutput").ap()
    gnn_kernel(nc, aps, out)
    r = run_bass_kernel_spmd(nc, [arrays], core_ids=[0])
    return r.results[0]["out_x"]
```
